# Optimizing a Trainium2 kernel written in Bass

```python
import numpy as np
import jax
import jax.numpy as jnp

def _softmax(x, axis=-1):
    return jax.nn.softmax(x, axis=axis)

def _gelu(x):
    return jax.nn.gelu(x, approximate=True)

def _silu(x):
    return jax.nn.silu(x)

def _sigmoid(x):
    return jax.nn.sigmoid(x)

def _layernorm(x, axis=-1, eps=1e-05):
    m = jnp.mean(x, axis=axis, keepdims=True)
    v = jnp.var(x, axis=axis, keepdims=True)
    return (x - m) / jnp.sqrt(v + eps)

def _scatter_add(tgt, idx, src, axis=0):
    return tgt.at[idx].add(src)

def _segment_sum(src, seg, n):
    return jax.ops.segment_sum(src, seg, n)
kernel_name = 'mk_adj_ffn_d1_adj_r2_ec72be'

def setup_inputs(seed: int=0):
    np.random.seed(seed)
    _w = jnp.asarray

    def _rec_inputs():
        import jax
        import jax.numpy as jnp
        _gk = jax.random.key(seed)
        x = -0.0005207 + 1.001 * jax.random.normal(jax.random.fold_in(_gk, 1), (1354, 256), jnp.float32)
        _w = (1.0 + jnp.arange(1354, dtype=jnp.float32)) ** (-0.5)
        _w = _w / _w.mean()
        _pij = jnp.clip(0.0118168 * _w[:, None] * _w[None, :], 0.0, 1.0)
        _a = jax.random.uniform(jax.random.fold_in(_gk, 2), (1354, 1354)) < _pij
        _af = _a.astype(jnp.float32)
        adj = _af
        return (x, adj)
    x, adj = _rec_inputs()

    def _L0_gnn_setup():
        import jax, jax.numpy as jnp
        import numpy as np
        ALPHA = 0.2
        NEG_INF = -1000000000000.0
        key = jax.random.key(seed)
        k1, k2, k3, k4, k5 = jax.random.split(key, 5)
        N, F = (2048, 256)
        inp = jax.random.normal(k1, (N, F), dtype=jnp.float32)
        adj = jax.random.randint(k2, (N, N), 0, 2).astype(jnp.float32)
        W = jax.random.normal(k3, (F, F), dtype=jnp.float32) * (1.414 / np.sqrt(F))
        a = jax.random.normal(k4, (2 * F, 1), dtype=jnp.float32) * 0.05
        wtrans = jax.random.normal(k5, (2 * F, F), dtype=jnp.float32) * (1.414 / np.sqrt(1.5 * F))
        return {'inp': inp, 'adj': adj, 'W': W, 'a': a, 'wtrans': wtrans}
    _L0_gnn_all = _L0_gnn_setup()
    _L0_gnn_in = {k: v for k, v in _L0_gnn_all.items() if k in ('W', 'a', 'wtrans')}
    del _L0_gnn_all

    def _L0_ffn_setup():
        import jax, jax.numpy as jnp
        import numpy as np
        B, T, C = (8, 512, 256)
        H = 512
        G, EG = (2, 4)
        E = G * EG
        K = 2
        LN_EPS = 1e-05

        def _swiglu(x):
            a, b = jnp.split(x, 2, axis=-1)
            return jax.nn.silu(a) * b
        key = jax.random.key(seed)
        ks = jax.random.split(key, 8)
        n = lambda k, shape, s: jax.random.normal(k, shape, dtype=jnp.float32) * s
        return {'x': n(ks[0], (B, T, C), 1.0), 'ln_scale': jnp.ones((C,), jnp.float32), 'ln_bias': jnp.zeros((C,), jnp.float32), 'shared_in_w': n(ks[1], (2 * H, C), 0.02), 'shared_out_w': n(ks[2], (C, H), 0.02), 'shared_out_b': jnp.zeros((C,), jnp.float32), 'expert_in_w': n(ks[3], (2 * H, C), 0.02), 'expert_out_weight': n(ks[4], (E, C, H), 0.02), 'expert_out_bias': jnp.zeros((E, C), jnp.float32), 'group_gate_w': n(ks[5], (G, C), 0.02), 'expert_gate_w': n(ks[6], (E, C), 0.02), 'group_bias': jnp.zeros((G,), jnp.float32), 'expert_bias': jnp.zeros((E,), jnp.float32)}
    _L0_ffn_all = _L0_ffn_setup()
    _L0_ffn_in = {k: v for k, v in _L0_ffn_all.items() if k in ('ln_scale', 'ln_bias', 'shared_in_w', 'shared_out_w', 'shared_out_b', 'expert_in_w', 'expert_out_weight', 'expert_out_bias', 'group_gate_w', 'expert_gate_w', 'group_bias', 'expert_bias')}
    del _L0_ffn_all
    return {'x': x, 'adj': adj, 'L0_gnn_W': _L0_gnn_in['W'], 'L0_gnn_a': _L0_gnn_in['a'], 'L0_gnn_wtrans': _L0_gnn_in['wtrans'], 'L0_ffn_ln_scale': _L0_ffn_in['ln_scale'], 'L0_ffn_ln_bias': _L0_ffn_in['ln_bias'], 'L0_ffn_shared_in_w': _L0_ffn_in['shared_in_w'], 'L0_ffn_shared_out_w': _L0_ffn_in['shared_out_w'], 'L0_ffn_shared_out_b': _L0_ffn_in['shared_out_b'], 'L0_ffn_expert_in_w': _L0_ffn_in['expert_in_w'], 'L0_ffn_expert_out_weight': _L0_ffn_in['expert_out_weight'], 'L0_ffn_expert_out_bias': _L0_ffn_in['expert_out_bias'], 'L0_ffn_group_gate_w': _L0_ffn_in['group_gate_w'], 'L0_ffn_expert_gate_w': _L0_ffn_in['expert_gate_w'], 'L0_ffn_group_bias': _L0_ffn_in['group_bias'], 'L0_ffn_expert_bias': _L0_ffn_in['expert_bias']}

def reference(x, adj, L0_gnn_W, L0_gnn_a, L0_gnn_wtrans, L0_ffn_ln_scale, L0_ffn_ln_bias, L0_ffn_shared_in_w, L0_ffn_shared_out_w, L0_ffn_shared_out_b, L0_ffn_expert_in_w, L0_ffn_expert_out_weight, L0_ffn_expert_out_bias, L0_ffn_group_gate_w, L0_ffn_expert_gate_w, L0_ffn_group_bias, L0_ffn_expert_bias):
    import jax
    import jax.numpy as jnp

    def _L0_gnn_ref(inp, adj, W, a, wtrans):
        import jax, jax.numpy as jnp
        import numpy as np
        ALPHA = 0.2
        NEG_INF = -1000000000000.0
        F_out = W.shape[1]
        h = inp @ W
        Wh1 = h @ a[:F_out, :]
        Wh2 = h @ a[F_out:, :]
        e = jax.nn.leaky_relu(Wh1 + Wh2.T, ALPHA)
        mask = adj > 0
        attention = jax.nn.softmax(jnp.where(mask, e, NEG_INF), axis=1)
        negative_attention = -jax.nn.softmax(jnp.where(mask, -e, NEG_INF), axis=1)
        h_prime = attention @ inp
        h_prime_negative = negative_attention @ inp
        h_prime_double = jnp.concatenate([h_prime, h_prime_negative], axis=1)
        new_h_prime = h_prime_double @ wtrans
        return jax.nn.elu(new_h_prime)

    def _L0_ffn_ref(x, ln_scale, ln_bias, shared_in_w, shared_out_w, shared_out_b, expert_in_w, expert_out_weight, expert_out_bias, group_gate_w, expert_gate_w, group_bias, expert_bias):
        import jax, jax.numpy as jnp
        import numpy as np
        B, T, C = (8, 512, 256)
        H = 512
        G, EG = (2, 4)
        E = G * EG
        K = 2
        LN_EPS = 1e-05

        def _swiglu(x):
            a, b = jnp.split(x, 2, axis=-1)
            return jax.nn.silu(a) * b
        Bx, Tx, Cx = x.shape
        S = Bx * Tx
        flat = x.reshape(S, Cx)
        mu = flat.mean(-1, keepdims=True)
        var = ((flat - mu) ** 2).mean(-1, keepdims=True)
        flat = (flat - mu) * jax.lax.rsqrt(var + LN_EPS) * ln_scale + ln_bias
        h_shared = _swiglu(flat @ shared_in_w.T)
        out_shared = h_shared @ shared_out_w.T + shared_out_b
        g_logits = flat @ group_gate_w.T + group_bias
        g_idx = jnp.argmax(g_logits, axis=-1)
        e_logits = (flat @ expert_gate_w.T).reshape(S, G, EG)
        e_sel = jnp.take_along_axis(e_logits, g_idx[:, None, None], axis=1)[:, 0, :]
        e_sel = e_sel + expert_bias.reshape(G, EG)[g_idx]
        e_probs = jax.nn.softmax(e_sel, axis=-1)
        topv, topi = jax.lax.top_k(e_probs, K)
        topv = topv / (topv.sum(-1, keepdims=True) + 1e-08)
        disp = g_idx[:, None] * EG + topi
        h_expert = _swiglu(flat @ expert_in_w.T)
        rows = jnp.arange(S)[:, None]
        comb = jnp.zeros((S, E), flat.dtype).at[rows, disp].add(topv)
        cnt = jnp.zeros((S, E), flat.dtype).at[rows, disp].add(1.0)
        routed = cnt @ expert_out_bias
        for e in range(E):
            routed = routed + comb[:, e:e + 1] * (h_expert @ expert_out_weight[e].T)
        return (out_shared + routed).reshape(Bx, Tx, Cx)
    x = x + _L0_gnn_ref(_layernorm(x, axis=-1), adj, L0_gnn_W, L0_gnn_a, L0_gnn_wtrans)
    x = x + _L0_ffn_ref(_layernorm(x, axis=-1)[None], L0_ffn_ln_scale, L0_ffn_ln_bias, L0_ffn_shared_in_w, L0_ffn_shared_out_w, L0_ffn_shared_out_b, L0_ffn_expert_in_w, L0_ffn_expert_out_weight, L0_ffn_expert_out_bias, L0_ffn_group_gate_w, L0_ffn_expert_gate_w, L0_ffn_group_bias, L0_ffn_expert_bias)[0]
    return x

_drawn_inputs = setup_inputs


def setup_inputs(seed=0):
    import zlib

    import numpy as np

    out = dict(_drawn_inputs(seed))
    spreads = {'L0_ffn_ln_scale': (1.0, 0.2),
     'L0_ffn_ln_bias': (0.0, 0.1),
     'L0_ffn_shared_out_b': (0.0, 0.1),
     'L0_ffn_expert_out_bias': (0.0, 0.1),
     'L0_ffn_group_bias': (0.0, 0.1),
     'L0_ffn_expert_bias': (0.0, 0.1)}
    factors = {'L0_ffn_expert_in_w': 3.454, 'L0_ffn_expert_out_weight': 3.456, 'L0_ffn_shared_in_w': 2.74}
    for name, (base, spread) in spreads.items():
        noise = np.random.default_rng([zlib.crc32(name.encode()), seed]).standard_normal(out[name].shape)
        drawn = base * np.exp(spread * noise) if base else spread * noise
        out[name] = jnp.asarray(drawn.astype(out[name].dtype))
    for name, factor in factors.items():
        out[name] = (out[name] * factor).astype(out[name].dtype)
    return out
```

```python
from contextlib import ExitStack

import concourse.bass as bass
from concourse import mybir

P = 128
F32 = mybir.dt.float32
F16 = mybir.dt.float16
BF16 = mybir.dt.bfloat16
ALU = mybir.AluOpType
ACT = mybir.ActivationFunctionType
AX_X = mybir.AxisListType.X

BIG = 1e30
NO_NEIGHBOUR = -1e29
SLOPE = 0.2
EPS = 1e-5
TOP_EPS = 1e-8
X_SCALE = 2.0 ** 5
W_SCALE = 2.0 ** 8
V_SCALE = 2.0 ** 6
P_LOG_SCALE = 9.010913347279288
H_SCALE = 2.0 ** 4
CNT_SCALE = 2.0 ** 6

PREP_STEPS = 9
TAIL_STEPS = 7
GATE_STEPS = 10
SWIGLU_STEPS = 2


def gnn_moe_kernel(nc, x, adj, gat_w, gat_a, wtrans, ln_pair, sh_in, sh_out, sh_out_b,
                   ex_in, ex_out, ex_out_b, group_gate, expert_gate, group_bias, expert_bias, out):
    N, C = x.shape
    T = -(-N // P)
    NP = T * P
    LAST = N - (T - 1) * P
    KC = C // P
    H = sh_out.shape[0]
    KH = H // P
    E = ex_out.shape[1]
    G = group_gate.shape[1]
    EG = E // G
    VW = C + 1
    ROWS = 7
    UNITS = [(0, 4), (4, 4), (8, T - 8)]
    NU = len(UNITS)
    NPAIR = E // 2
    TAIL = [((T - 1) * P, 0, 64), ((T - 1) * P + 64, 64, LAST - 64)]
    assert C == 256 and KH == 4 and E == 8 and T == 11 and LAST > 64

    with ExitStack() as ctx:
        def sb(name, shape, dt=F32):
            return ctx.enter_context(nc.sbuf_tensor(name, shape, dt))

        def sem(name):
            return ctx.enter_context(nc.semaphore(name))

        xall = sb("xall", [P, T, C])
        ramp = sb("ramp", [P, T, NP])
        v_hi = sb("v_hi", [P, T, 2, VW + 1], F16)
        v_lo = sb("v_lo", [P, T, 2, C], F16)
        t_row = sb("t_row", [P, NP])
        st_col = sb("st_col", [P, T, 2])
        in_hi = sb("in_hi", [P, 2, KC, 2 * H], F16)
        in_lo = sb("in_lo", [P, 2, KC, 2 * H], F16)
        so_hi = sb("so_hi", [P, KH, C], F16)
        so_lo = sb("so_lo", [P, KH, C], F16)
        ew = sb("ew", [P, 2, KH, E * C], F16)
        gates = sb("gates", [P, KC, G + E])
        gate_bias = sb("gate_bias", [P, G + E])
        lnsb = sb("lnsb", [P, 2, KC])
        bias_rows = sb("bias_rows", [E + 1, C])
        bias_hi = sb("bias_hi", [E + 1, C], F16)
        bias_lo = sb("bias_lo", [E + 1, C], F16)
        mean_hi = sb("mean_hi", [ROWS, 2, VW + 1], F16)
        mean_lo = sb("mean_lo", [ROWS, 2, C], F16)
        mean_w = sb("mean_w", [P, ROWS], F16)
        ident_b = sb("ident_b", [P, P], BF16)
        ident_h = sb("ident_h", [P, P], F16)
        ident_f = sb("ident_f", [P, P])
        t_parts = sb("t_parts", [P, T, 6], BF16)
        t_rows = sb("t_rows", [6, T, P], BF16)
        t_ramp = sb("t_ramp", [P, T])
        slope_s = sb("slope_s", [P, T])
        one_col = sb("one_col", [P, 1])
        neg_half = sb("neg_half", [P, T])
        signs = sb("signs", [P, 2])
        unscale = sb("unscale", [P, 2])
        earlier = sb("earlier", [P, E, E])
        adj_sb = sb("adj_sb", [P, N])
        madj = sb("madj", [P, NP], BF16)
        ttr_out = sb("ttr_out", [P, N], BF16)
        stat = sb("stat", [P, 16])
        mcol = sb("mcol", [P, 2, ROWS], BF16)
        mrow = sb("mrow", [ROWS, 2, P], BF16)
        prob = sb("prob", [P, 2, 2, 4 * P])
        p_hi = sb("p_hi", [P, NU, 2, 4 * P], F16)
        p_lo = sb("p_lo", [P, NU, 2, 4 * P], F16)
        tail_sb = sb("tail_sb", [P, 4, C])
        new, elu, x1, y = (tail_sb[:, n, :] for n in range(4))
        bn = sb("bn", [P, 6])
        mv = sb("mv", [P, 4])
        carrier = sb("carrier", [1, 1])
        flat = sb("flat", [P, KC, P])
        flat_hi = sb("flat_hi", [P, KC, P], F16)
        flat_lo = sb("flat_lo", [P, KC, P], F16)
        gl = sb("gl", [P, G + E])
        pen = sb("pen", [P, G])
        z8 = sb("z8", [P, E])
        cmp_gt = sb("cmp_gt", [P, E, E])
        cmp_eq = sb("cmp_eq", [P, E, E])
        route = sb("route", [P, 8])
        e8 = sb("e8", [P, E])
        picked = sb("picked", [P, E])
        comb = sb("comb", [P, E])
        cnt = sb("cnt", [P, E + 2], F16)
        cnt_t = sb("cnt_t", [E + 1, P], F16)
        gact_hid = sb("gact_hid", [P, 2, KH * P])
        gact, hid = gact_hid[:, 0, :], gact_hid[:, 1, :]
        h_parts = sb("h_parts", [P, 2, 2, KH, P], F16)
        h_hi, h_lo = h_parts[:, 0, :, :, :], h_parts[:, 1, :, :, :]
        acc_o = sb("acc_o", [P, C])
        stage = [gact_hid[:, :, :].rearrange("p a n -> p (a n)"),
                 h_parts[:, :, :, :, :].rearrange("p a w k n -> p (a w k n)").bitcast(F32)]
        startup = ew[:, :, :, :].rearrange("p a k n -> p (a k n)")

        def carve(at, n, dt):
            size = 4 if dt == F32 else 2
            view = startup[:, at // 2:(at + n * size) // 2]
            return (view.bitcast(F32) if dt == F32 else view), at + n * size

        inp_t, at = carve(0, KC * NP, F32)
        inp_hi, at = carve(at, KC * NP, F16)
        inp_lo, at = carve(at, KC * NP, F16)
        assert at <= 2 * KH * E * C * 2
        inp_t, inp_hi, inp_lo = (v.rearrange("p (k n) -> p k n", k=KC) for v in (inp_t, inp_hi, inp_lo))
        wt_hi = p_hi[:, 0, :, :].rearrange("p a (b c) -> p (a b) c", c=C)
        wt_lo = p_lo[:, 0, :, :].rearrange("p a (b c) -> p (a b) c", c=C)
        inp = prob[:, 0, :, :].rearrange("p a (b c) -> p (a b) c", c=C)
        gw_sb = p_hi[:, 1, :, :].rearrange("p a b -> p (a b)").bitcast(F32).rearrange("p (k c) -> p k c", k=KC)
        ga_sb = p_lo[:, 1, :, :].rearrange("p a b -> p (a b)").bitcast(F32).rearrange("p (k c) -> p k c", k=2)
        wa_rep = prob[:, 1, :, :].rearrange("p a (b c) -> p a b c", c=P)
        t_rest = tail_sb[:, 1, 0:2 * T].rearrange("p (a t) -> p a t", t=T)
        mean_f = tail_sb[0:ROWS, 2:4, :]
        wa = sb("wa", [P, KC, 2])
        bn0 = sb("bn0", [P, T, 6])
        mv0 = sb("mv0", [P, T, 2])
        rs0 = sb("rs0", [P, T])
        wa_out = new

        psum = ctx.enter_context(nc.psum_tensor("psum", [P, 8, 512], F32))
        q_ps = [psum[:, 0, :], psum[:, 1, :]]
        acc_ps = [psum[:, 2, :], psum[:, 3, :]]
        f_ps = [psum[:, 4 + i, :] for i in range(4)]
        s_ps = psum[:, 2:5, :].rearrange("p b n -> p (b n)")
        t_ps = psum[:, 5:8, :].rearrange("p b n -> p (b n)")
        tr_ps = [psum[:, 0, 0:KC * P], psum[:, 1, 0:KC * P]]
        v_ps = [psum[:, 0, :], psum[:, 1, :]]
        mean_ps = psum[0:ROWS, 6, :]
        mrow_ps = f_ps[1].bitcast(BF16)
        t_rows_ps = psum[:, 6:8, :].rearrange("p b n -> p (b n)").bitcast(BF16)
        cnt_ps = f_ps[2].bitcast(F16)

        x_in = [sem(f"x_in{i}") for i in range(3)]
        gat_in = sem("gat_in")
        small_in = sem("small_in")
        staged = [sem("staged0"), sem("staged1")]
        x_pad = sem("x_pad")
        consts = sem("consts")
        pool_chain = sem("pool_chain")
        stats0 = sem("stats0")
        rstd0 = sem("rstd0")
        start_chain = sem("start_chain")
        wa_ready = sem("wa_ready")
        inp_ready = sem("inp_ready")
        inp_tr = sem("inp_tr")
        inp_f = sem("inp_f")
        inp_l = sem("inp_l")
        st_ready = sem("st_ready")
        tcols = sem("tcols")
        ramp_ready = sem("ramp_ready")
        v_mm = sem("v_mm")
        vh_done = sem("vh_done")
        vl_done = sem("vl_done")
        t_rows_tr = sem("t_rows_tr")
        t_rows_done = sem("t_rows_done")
        mean_mm = sem("mean_mm")
        mean_done = sem("mean_done")
        w_hi = sem("w_hi")
        w_lo = sem("w_lo")
        bias_done = sem("bias_done")
        ln_scaled = sem("ln_scaled")
        adj_in = sem("adj_in")
        madj_ready = sem("madj_ready")
        prep_chain = sem("prep_chain")
        mcol_ready = sem("mcol_ready")
        mrow_tr = sem("mrow_tr")
        mrow_ready = sem("mrow_ready")
        q_ready = [sem("q_ready0"), sem("q_ready1")]
        z_done = [sem("z_done0"), sem("z_done1")]
        exp_done = sem("exp_done")
        phi_done = sem("phi_done")
        plo_done = sem("plo_done")
        att_done = sem("att_done")
        tail_chain = sem("tail_chain")
        acc_used = sem("acc_used")
        new_neg = sem("new_neg")
        elu_exp = sem("elu_exp")
        stats1 = sem("stats1")
        rstd1 = sem("rstd1")
        y_ready = sem("y_ready")
        flat_tr = sem("flat_tr")
        flat_f = sem("flat_f")
        flat_h = sem("flat_h")
        flat_l = sem("flat_l")
        logits = sem("logits")
        gl_done = sem("gl_done")
        gate_chain = sem("gate_chain")
        swiglu_chain = sem("swiglu_chain")
        negmax = sem("negmax")
        e8_done = sem("e8_done")
        cnt_ready = sem("cnt_ready")
        cnt_tr = sem("cnt_tr")
        cnt_copied = sem("cnt_copied")
        in_mm = [sem("in_mm_shared"), sem("in_mm_expert")]
        tanh_done = [sem("tanh_shared"), sem("tanh_expert")]
        hid_done = [sem("hid_shared"), sem("hid_expert")]
        hhi_done = [sem("hhi_shared"), sem("hhi_expert")]
        hlo_done = [sem("hlo_shared"), sem("hlo_expert")]
        so_mm = sem("so_mm")
        so_used = sem("so_used")
        comb_ready = sem("comb_ready")
        half_added = sem("half_added")
        pair_mm = sem("pair_mm")
        pair_used = sem("pair_used")
        out_stored = sem("out_stored")

        def after(eng, s, n):
            if not isinstance(n, int) or n > 0:
                eng.wait_ge(s, n)

        def hold():
            nc.vector.memset(carrier[:, :], 0.0)

        class Chain:
            def __init__(self, eng, s, per_tile):
                self.eng, self.s, self.per_tile = eng, s, per_tile

            def tile(self, t):
                self.t, self.k = t, 0

            def link(self, ins):
                self.k += 1
                ins.then_inc(self.s, 1)
                self.eng.wait_ge(self.s, self.t * self.per_tile + self.k)

            def done(self):
                assert self.k == self.per_tile, (self.s, self.k)

        def weight_list():
            lst = [(wtrans.rearrange("(b p) c -> p b c", p=P), wt_hi, wt_lo)]
            for w, src in ((0, sh_in), (1, ex_in)):
                for k in range(KC):
                    lst.append((src[k * P:(k + 1) * P, :], in_hi[:, w, k, :], in_lo[:, w, k, :]))
            lst.append((sh_out.rearrange("(k p) c -> p k c", p=P), so_hi[:, :, :], so_lo[:, :, :]))
            for k in range(KH):
                for half in range(2):
                    e = slice(half * E // 2, (half + 1) * E // 2)
                    c = slice(half * E // 2 * C, (half + 1) * E // 2 * C)
                    lst.append((ex_out[k * P:(k + 1) * P, e, :], ew[:, 0, k, c], ew[:, 1, k, c]))
            return lst

        weights = weight_list()

        def stage_view(n, like):
            v = stage[n % 2]
            if len(like.shape) == 2:
                return v
            return v.rearrange("p (a b) -> p a b", b=like.shape[2])

        def flat_free(ap):
            return ap if len(ap.shape) == 2 else ap.rearrange("p a b -> p (a b)")

        block = ctx.enter_context(nc.Block())

        @block.sync
        def _(sp):
            sp.dma_start(xall[:, 0:4, :], x[0:4 * P, :].rearrange("(t p) c -> p t c", p=P)).then_inc(x_in[0], 16)
            sp.dma_start(gw_sb, gat_w.rearrange("(k p) c -> p k c", p=P)).then_inc(gat_in, 16)
            sp.dma_start(ga_sb, gat_a.partition_broadcast(P)).then_inc(gat_in, 16)
            sp.dma_start(xall[:, 4:T - 1, :], x[4 * P:(T - 1) * P, :].rearrange("(t p) c -> p t c", p=P)).then_inc(x_in[1], 16)
            sp.wait_ge(x_pad, 1)
            for row, part, n in TAIL:
                sp.dma_start(xall[part:part + n, T - 1, :], x[row:row + n, :]).then_inc(x_in[2], 16)
            def load_weight(n):
                src = weights[n][0]
                if n >= 2:
                    sp.wait_ge(w_lo, n - 1)
                sp.dma_start(stage_view(n, src), src).then_inc(staged[n % 2], 16)

            load_weight(0)
            sp.dma_start(adj_sb[:, :], adj[0:P, :]).then_inc(adj_in, 16)
            sp.dma_start(gates[:, :, 0:G], group_gate.rearrange("(k p) g -> p k g", p=P)).then_inc(small_in, 16)
            sp.dma_start(gates[:, :, G:G + E], expert_gate.rearrange("(k p) g -> p k g", p=P)).then_inc(small_in, 16)
            sp.dma_start(gate_bias[:, 0:G], group_bias.partition_broadcast(P)).then_inc(small_in, 16)
            sp.dma_start(gate_bias[:, G:G + E], expert_bias.partition_broadcast(P)).then_inc(small_in, 16)
            sp.dma_start(lnsb[:, :, :], ln_pair).then_inc(small_in, 16)
            sp.dma_start(bias_rows[0:E, :], ex_out_b).then_inc(small_in, 16)
            sp.dma_start(bias_rows[E:E + 1, :], sh_out_b.rearrange("(o c) -> o c", o=1)).then_inc(small_in, 16)
            load_weight(1)
            load_weight(2)
            sp.wait_ge(madj_ready, 1)
            sp.dma_start(adj_sb[:, :], adj[P:2 * P, :]).then_inc(adj_in, 16)
            for n in range(3, len(weights)):
                load_weight(n)

            def store(t, row, part, n):
                sp.wait_ge(pair_used, NPAIR * (t + 1))
                sp.dma_start(out[row:row + n, :] if isinstance(row, int) else out[bass.ds(row, n), :],
                             acc_o[part:part + n, :]).then_inc(out_stored, 16)

            with sp.Fori(1, T - 2) as t:
                sp.wait_ge(madj_ready, t + 1)
                sp.dma_start(adj_sb[:, :], adj[bass.ds((t + 1) * P, P), :]).then_inc(adj_in, 16)
                store(t - 1, (t - 1) * P, 0, P)
            sp.wait_ge(madj_ready, T - 1)
            for row, part, n in TAIL:
                sp.dma_start(adj_sb[part:part + n, :], adj[row:row + n, :]).then_inc(adj_in, 16)
            store(T - 3, (T - 3) * P, 0, P)
            store(T - 2, (T - 2) * P, 0, P)
            for row, part, n in TAIL:
                store(T - 1, row, part, n)
            sp.wait_ge(out_stored, 16 * (T + 1))

        @block.gpsimd
        def _(pool):
            nc.gpsimd.memset(xall[:, T - 1, :], 0.0).then_inc(x_pad, 1)
            steps = [0]

            def link(ins):
                steps[0] += 1
                ins.then_inc(pool_chain, 1)
                pool.wait_ge(pool_chain, steps[0])

            nc.gpsimd.memset(ident_b[:, :], 0.0)
            nc.gpsimd.memset(ident_h[:, :], 0.0)
            nc.gpsimd.memset(mean_w[:, :], 0.0)
            nc.gpsimd.memset(neg_half[:, :], -0.5)
            link(nc.gpsimd.memset(ident_f[:, :], 0.0))
            for m in (ident_f, ident_b, ident_h):
                nc.gpsimd.affine_select(out=m[:, :], in_=m[:, :], compare_op=ALU.not_equal, fill=1.0, base=0,
                                        pattern=[[-1, P]], channel_multiplier=1)
            nc.gpsimd.memset(mean_w[:, ROWS - 1:ROWS], 1.0)
            nc.gpsimd.memset(t_parts[:, :, 0:3], 1.0)
            nc.gpsimd.memset(mcol[:, 0, 3:6], 1.0)
            nc.gpsimd.memset(mcol[:, 1, 3:6], -1.0)
            nc.gpsimd.memset(one_col[:, :], 1.0)
            nc.gpsimd.memset(signs[:, 0:1], -1.0)
            nc.gpsimd.memset(signs[:, 1:2], 1.0)
            nc.gpsimd.memset(unscale[:, 0:1], 1.0 / V_SCALE)
            nc.gpsimd.memset(unscale[:, 1:2], -1.0 / V_SCALE)
            nc.gpsimd.memset(cnt[:, :], CNT_SCALE)
            nc.gpsimd.memset(mean_hi[:, :, :], 0.0)
            nc.gpsimd.memset(v_hi[:, :, :, C:VW + 1], 1.0)
            nc.gpsimd.memset(madj[:, N:NP], -BIG)
            nc.gpsimd.memset(t_row[:, N:NP], 0.0)
            link(nc.gpsimd.memset(earlier[:, :, :], 1.0))
            nc.gpsimd.affine_select(out=earlier[:, :, :], in_=earlier[:, :, :], compare_op=ALU.is_gt, fill=0.0,
                                    base=0, pattern=[[1, E], [-1, E]], channel_multiplier=0).then_inc(consts, 1)
            for n, (a, b) in enumerate(((0, 4), (4, T - 1), (T - 1, T))):
                pool.wait_ge(stats0, b)
                link(nc.gpsimd.tensor_scalar(rs0[:, a:b], mv0[:, a:b, 1], EPS, None, ALU.add))
                nc.gpsimd.tensor_tensor(rs0[:, a:b], rs0[:, a:b], neg_half[:, a:b], ALU.pow).then_inc(rstd0, 1)
            def rstd(t):
                pool.wait_ge(stats1, t + 1)
                nc.gpsimd.tensor_tensor(mv[:, 3:4], mv[:, 2:3], neg_half[:, 0:1], ALU.pow).then_inc(rstd1, 1)

            def flat_low(t):
                pool.wait_ge(flat_h, t + 1)
                nc.gpsimd.tensor_tensor(flat_lo[:, :, :], flat[:, :, :], flat_hi[:, :, :], ALU.subtract).then_inc(flat_l, 1)

            def hid_low(t, w):
                pool.wait_ge(hhi_done[w], t + 1)
                nc.gpsimd.tensor_tensor(h_lo[:, w, :, :], hid[:, :].rearrange("p (k n) -> p k n", k=KH),
                                        h_hi[:, w, :, :], ALU.subtract).then_inc(hlo_done[w], 1)

            def ffn(t):
                flat_low(t)
                hid_low(t, 0)
                hid_low(t, 1)

            rstd(0)
            with pool.Fori(1, T) as t:
                ffn(t - 1)
                rstd(t)
            ffn(T - 1)

        @block.scalar
        def _(act):
            def weight_hi(n):
                src, hi, _ = weights[n]
                act.wait_ge(staged[n % 2], 16 * (n // 2 + 1))
                nc.scalar.activation(flat_free(hi), stage[n % 2], ACT.Copy, scale=W_SCALE).then_inc(w_hi, 1)

            weight_hi(0)
            for t in range(T):
                act.wait_ge(inp_tr, t + 1)
                ps = tr_ps[t % 2].rearrange("p (k n) -> p k n", k=KC)
                nc.scalar.activation(inp_hi[:, :, t * P:(t + 1) * P], ps, ACT.Copy, scale=X_SCALE)
                nc.scalar.activation(inp_t[:, :, t * P:(t + 1) * P], ps, ACT.Copy).then_inc(inp_f, 1)
            act.wait_ge(st_ready, 1)
            act.wait_ge(tcols, 2)
            for j in range(T):
                nc.scalar.activation(ramp[:, j, :], s_ps[:, 0:NP], ACT.Relu, bias=t_ramp[:, j:j + 1], scale=1.0 - SLOPE).then_inc(ramp_ready, 1)
                act.wait_ge(v_mm, j + 1)
                nc.scalar.activation(v_hi[:, j, :, 0:C], v_ps[j % 2].rearrange("p (s c) -> p s c", s=2), ACT.Copy,
                                     scale=V_SCALE / (X_SCALE * W_SCALE)).then_inc(vh_done, 1)

            def exps(t, u):
                w = UNITS[u][1] * P
                for s in range(2):
                    act.wait_ge(z_done[s], NU * t + u + 1)
                pr = prob[:, u % 2, :, 0:w]
                nc.scalar.activation(pr, pr, ACT.Exp).then_inc(exp_done, 1)

            def highs(t, u):
                w = UNITS[u][1] * P
                act.wait_ge(exp_done, NU * t + u + 1)
                after(act, att_done, NU * (t - 1) + u + 1)
                nc.scalar.activation(p_hi[:, u, :, 0:w], prob[:, u % 2, :, 0:w], ACT.Copy).then_inc(phi_done, 1)

            def mrow_copy(t):
                act.wait_ge(mrow_tr, t + 1)
                nc.scalar.activation(mrow[:, :, :], mrow_ps[0:ROWS, 0:2 * P].rearrange("p (s n) -> p s n", s=2), ACT.Copy).then_inc(mrow_ready, 1)

            def elu_part(t):
                act.wait_ge(new_neg, t + 1)
                nc.scalar.activation(elu[:, :], elu[:, :], ACT.Exp).then_inc(elu_exp, 1)

            def flat_part(t):
                act.wait_ge(flat_tr, t + 1)
                ps = f_ps[0][:, 0:KC * P].rearrange("p (k n) -> p k n", k=KC)
                after(act, flat_l, t)
                for k in range(KC):
                    nc.scalar.activation(flat[:, k, :], ps[:, k, :], ACT.Identity, bias=lnsb[:, 1, k:k + 1],
                                         scale=lnsb[:, 0, k:k + 1]).then_inc(flat_f, 1)
                act.wait_ge(flat_f, KC * (t + 1))
                nc.scalar.activation(flat_hi[:, :, :], flat[:, :, :], ACT.Copy).then_inc(flat_h, 1)

            def tanhs(t, w):
                act.wait_ge(in_mm[w], t + 1)
                nc.scalar.activation(gact[:, :], f_ps[2 - 2 * w], ACT.Tanh, scale=0.5 / (X_SCALE * W_SCALE)).then_inc(tanh_done[w], 1)

            def hid_high(t, w):
                act.wait_ge(hid_done[w], t + 1)
                after(act, *((so_mm, t) if w == 0 else (pair_mm, NPAIR * t)))
                nc.scalar.activation(h_hi[:, w, :, :], hid[:, :].rearrange("p (k n) -> p k n", k=KH), ACT.Copy).then_inc(hhi_done[w], 1)

            def route_exp(t):
                act.wait_ge(negmax, t + 1)
                nc.scalar.activation(e8[:, :], z8[:, :], ACT.Exp, bias=route[:, 0:1], accum_out=route[:, 1:2]).then_inc(e8_done, 1)

            def tile(t, attn, ffn, more):
                f = t - 1
                if attn:
                    exps(t, 0)
                if ffn:
                    flat_part(f)
                if attn:
                    highs(t, 0)
                if not ffn:
                    act.wait_ge(mean_done, 1)
                    nc.scalar.activation(mean_hi[:, :, 0:C], mean_f[:, :, :], ACT.Copy).then_inc(mean_done, 1)
                if ffn:
                    route_exp(f)
                    tanhs(f, 0)
                    hid_high(f, 0)
                if attn:
                    exps(t, 1)
                    highs(t, 1)
                if ffn:
                    tanhs(f, 1)
                    hid_high(f, 1)
                if attn:
                    exps(t, 2)
                    highs(t, 2)
                    if more:
                        mrow_copy(t + 1)
                    elu_part(t)

            act.wait_ge(t_rows_tr, 1)
            nc.scalar.activation(t_rows[:, :, :], t_rows_ps[0:6, 0:NP].rearrange("p (t n) -> p t n", n=P), ACT.Copy).then_inc(t_rows_done, 1)
            mrow_copy(0)
            tile(0, True, False, True)
            for n in range(1, len(weights)):
                weight_hi(n)
            act.wait_ge(small_in, 7 * 16)
            nc.scalar.activation(bias_hi[:, :], bias_rows[:, :], ACT.Copy, scale=H_SCALE * W_SCALE / CNT_SCALE).then_inc(bias_done, 1)
            act.wait_ge(ln_scaled, 1)
            tile(1, True, True, True)
            with act.Fori(2, T - 1) as t:
                tile(t, True, True, True)
            tile(T - 1, True, True, False)
            tile(T, False, True, False)

        @block.vector
        def _(dve):
            steps = [0]

            def link(ins):
                steps[0] += 1
                ins.then_inc(start_chain, 1)
                dve.wait_ge(start_chain, steps[0])

            def weight_lo(n):
                _, hi, lo = weights[n]
                dve.wait_ge(w_hi, n + 1)
                nc.vector.scalar_tensor_tensor(out=flat_free(lo), in0=stage[n % 2], scalar=W_SCALE, in1=flat_free(hi),
                                               op0=ALU.mult, op1=ALU.subtract).then_inc(w_lo, 1)

            dve.wait_ge(gat_in, 32)
            for k in range(KC):
                for s in range(2):
                    link(nc.vector.tensor_tensor_reduce(out=wa_out[:, :], in0=gw_sb[:, k, :], in1=ga_sb[:, s, :], scale=1.0,
                                                        scalar=0.0, op0=ALU.mult, op1=ALU.add, accum_out=wa[:, k, s:s + 1]))
            for k in range(KC):
                for s in range(2):
                    ins = nc.vector.tensor_copy(wa_rep[:, s, k, :], wa[:, k, s:s + 1].broadcast_to((P, P)))
            ins.then_inc(wa_ready, 1)
            ready = {0: 16, 4: 16, T - 1: 32}
            part = {0: 0, 4: 1, T - 1: 2}
            for t in range(T):
                if t in ready:
                    dve.wait_ge(x_in[part[t]], ready[t])
                link(nc.vector.bn_stats(bn0[:, t, :], xall[:, t, :]))
                nc.vector.bn_aggr(mv0[:, t, :], bn0[:, t, :]).then_inc(stats0, 1)
            weight_lo(0)

            def inp_low(t):
                dve.wait_ge(inp_f, t + 1)
                nc.vector.scalar_tensor_tensor(out=inp_lo[:, :, t * P:(t + 1) * P],
                                               in0=inp_t[:, :, t * P:(t + 1) * P], scalar=X_SCALE,
                                               in1=inp_hi[:, :, t * P:(t + 1) * P], op0=ALU.mult, op1=ALU.subtract).then_inc(inp_l, 1)

            for t in range(T):
                if t in ready:
                    dve.wait_ge(rstd0, part[t] + 1)
                if t >= 4:
                    dve.wait_ge(inp_tr, t - 3)
                nc.vector.tensor_scalar(inp[:, t % 4, :], xall[:, t, :], mv0[:, t, 0:1], rs0[:, t:t + 1],
                                        ALU.subtract, ALU.mult).then_inc(inp_ready, 1)
                if t >= 1:
                    inp_low(t - 1)
            inp_low(T - 1)
            dve.wait_ge(st_ready, 1)
            nc.vector.tensor_copy(st_col[:, :, :], t_ps[:, NP:NP + 2 * T].rearrange("p (t s) -> p t s", s=2)).then_inc(tcols, 1)
            dve.wait_ge(tcols, 1)
            nc.vector.tensor_scalar(t_ramp[:, :], st_col[:, :, 1], 1.0 - SLOPE, None, ALU.mult).then_inc(tcols, 1)
            nc.vector.tensor_scalar(slope_s[:, :], st_col[:, :, 0], -SLOPE, None, ALU.mult)
            r, q = t_rest[:, 0, :], t_rest[:, 1, :]
            dve.wait_ge(consts, 1)
            link(nc.vector.tensor_scalar(r, st_col[:, :, 1], SLOPE, None, ALU.mult))
            link(nc.vector.tensor_copy(t_parts[:, :, 3], r))
            link(nc.vector.tensor_tensor(q, r, t_parts[:, :, 3], ALU.subtract))
            link(nc.vector.tensor_copy(t_parts[:, :, 4], q))
            link(nc.vector.tensor_tensor(t_parts[:, :, 5], q, t_parts[:, :, 4], ALU.subtract))
            nc.vector.tensor_copy(t_row[:, 0:N], t_ps[:, 0:N]).then_inc(tcols, 1)

            prep = Chain(dve, prep_chain, PREP_STEPS)

            def column(cols, t):
                return cols[:, t:t + 1] if isinstance(t, int) else cols[:, bass.ds(t, 1)]

            def prepare(t, last=False):
                prep.tile(t)
                dve.wait_ge(adj_in, (T + 1) * 16 if last else (t + 1) * 16)
                after(dve, q_ready[1], NU * t)
                nc.vector.tensor_scalar(madj[:, 0:N], adj_sb[:, :], 0.0, -BIG, ALU.is_le, ALU.mult).then_inc(madj_ready, 1)
                dve.wait_ge(madj_ready, t + 1)
                hold()
                a, lr, q, r = stat[:, 0:2], stat[:, 2:4], stat[:, 4:6], stat[:, 6:8]
                top, neg_bottom = stat[:, 8:9], stat[:, 9:10]
                prep.link(nc.vector.tensor_tensor_reduce(out=ttr_out[:, :], in0=madj[:, 0:N], in1=t_row[:, 0:N], scale=1.0,
                                                         scalar=-2 * BIG, op0=ALU.add, op1=ALU.max, accum_out=top))
                hold()
                prep.link(nc.vector.tensor_tensor_reduce(out=ttr_out[:, :], in0=madj[:, 0:N], in1=t_row[:, 0:N], scale=1.0,
                                                         scalar=-2 * BIG, op0=ALU.subtract, op1=ALU.max, accum_out=neg_bottom))
                s = column(st_col[:, :, 0], t)
                nc.vector.tensor_tensor(stat[:, 0:1], top, s, ALU.add)
                nc.vector.tensor_scalar(mcol[:, 0, ROWS - 1:ROWS], top, NO_NEIGHBOUR, None, ALU.is_lt)
                nc.vector.tensor_scalar(mcol[:, 1, ROWS - 1:ROWS], top, NO_NEIGHBOUR, None, ALU.is_lt)
                prep.link(nc.vector.tensor_tensor(stat[:, 1:2], s, neg_bottom, ALU.subtract))
                prep.link(nc.vector.scalar_tensor_tensor(out=lr, in0=a, scalar=SLOPE, in1=a, op0=ALU.mult, op1=ALU.max))
                prep.link(nc.vector.scalar_tensor_tensor(out=r, in0=lr, scalar=column(slope_s, t), in1=signs[:, :], op0=ALU.add, op1=ALU.mult))
                prep.link(nc.vector.tensor_scalar(r, r, P_LOG_SCALE, None, ALU.add))
                prep.link(nc.vector.tensor_copy(mcol[:, :, 0], r))
                prep.link(nc.vector.tensor_tensor(q, r, mcol[:, :, 0], ALU.subtract))
                prep.link(nc.vector.tensor_copy(mcol[:, :, 1], q))
                nc.vector.tensor_tensor(mcol[:, :, 2], q, mcol[:, :, 1], ALU.subtract).then_inc(mcol_ready, 1)
                prep.done()

            def scores(t, u):
                j0, n = UNITS[u]
                w = n * P
                i = slice(t * P, (t + 1) * P) if isinstance(t, int) else bass.ds(t * P, P)
                after(dve, plo_done, (NU * t, NU * (t - 1) + 2, NU * t + 1)[u])
                for s in range(2):
                    dve.wait_ge(q_ready[s], NU * t + u + 1)
                    q3 = q_ps[s][:, 0:w].rearrange("p (j i) -> p j i", i=P)
                    o3 = prob[:, u % 2, s, 0:w].rearrange("p (j i) -> p j i", i=P)
                    nc.vector.tensor_tensor(o3, q3, ramp[:, j0:j0 + n, i], ALU.subtract if s else ALU.add).then_inc(z_done[s], 1)

            def lows(t, u):
                w = UNITS[u][1] * P
                dve.wait_ge(phi_done, NU * t + u + 1)
                nc.vector.tensor_tensor(p_lo[:, u, :, 0:w], prob[:, u % 2, :, 0:w], p_hi[:, u, :, 0:w], ALU.subtract).then_inc(plo_done, 1)

            tails = Chain(dve, tail_chain, TAIL_STEPS)

            def tail(t):
                tails.tile(t)
                dve.wait_ge(att_done, NU * (t + 1))
                nc.vector.reciprocal(stat[:, 12:13], acc_ps[0][:, C:VW])
                tails.link(nc.vector.reciprocal(stat[:, 13:14], acc_ps[1][:, C:VW]))
                tails.link(nc.vector.tensor_tensor(stat[:, 14:16], stat[:, 12:14], unscale[:, :], ALU.mult))
                tails.link(nc.vector.tensor_scalar(new[:, :], acc_ps[0][:, 0:C], stat[:, 14:15], None, ALU.mult))
                nc.vector.scalar_tensor_tensor(out=new[:, :], in0=acc_ps[1][:, 0:C], scalar=stat[:, 15:16], in1=new[:, :],
                                               op0=ALU.mult, op1=ALU.add).then_inc(acc_used, 1)
                dve.wait_ge(acc_used, t + 1)
                nc.vector.tensor_scalar(elu[:, :], new[:, :], 0.0, None, ALU.min).then_inc(new_neg, 1)
                xt = xall[:, t, :] if isinstance(t, int) else xall[:, bass.ds(t, 1), :].rearrange("p a c -> p (a c)")
                tails.link(nc.vector.scalar_tensor_tensor(out=x1[:, :], in0=new[:, :], scalar=0.0, in1=xt, op0=ALU.max, op1=ALU.add))
                dve.wait_ge(elu_exp, t + 1)
                tails.link(nc.vector.scalar_tensor_tensor(out=x1[:, :], in0=elu[:, :], scalar=-1.0, in1=x1[:, :], op0=ALU.add, op1=ALU.add))
                tails.link(nc.vector.bn_stats(bn[:, :], x1[:, :]))
                hold()
                tails.link(nc.vector.bn_aggr(mv[:, 0:2], bn[:, :]))
                nc.vector.tensor_scalar(mv[:, 2:3], mv[:, 1:2], 1.0 + EPS, EPS * EPS, ALU.mult, ALU.add).then_inc(stats1, 1)
                dve.wait_ge(rstd1, t + 1)
                after(dve, flat_tr, t)
                nc.vector.tensor_scalar(y[:, :], x1[:, :], mv[:, 0:1], mv[:, 3:4], ALU.subtract, ALU.mult).then_inc(y_ready, 1)
                tails.done()

            gates_c = Chain(dve, gate_chain, GATE_STEPS)

            def gate(t):
                gates_c.tile(t)
                dve.wait_ge(logits, t + 1)
                nc.vector.scalar_tensor_tensor(out=gl[:, :], in0=f_ps[1][:, 0:G + E], scalar=1.0 / X_SCALE, in1=gate_bias[:, :],
                                               op0=ALU.mult, op1=ALU.add).then_inc(gl_done, 1)
                dve.wait_ge(gl_done, t + 1)
                nc.vector.tensor_scalar(pen[:, 0:1], gl[:, 1:2], gl[:, 0:1], -BIG, ALU.is_gt, ALU.mult)
                gates_c.link(nc.vector.tensor_scalar(pen[:, 1:2], gl[:, 1:2], gl[:, 0:1], -BIG, ALU.is_le, ALU.mult))
                for g in range(G):
                    e = slice(g * EG, (g + 1) * EG)
                    ins = nc.vector.tensor_scalar(z8[:, e], gl[:, G + g * EG:G + (g + 1) * EG], pen[:, g:g + 1], None, ALU.add)
                gates_c.link(ins)
                nc.vector.tensor_reduce(route[:, 0:1], z8[:, :], AX_X, ALU.max, negate=True).then_inc(negmax, 1)
                z_j = z8[:, :].unsqueeze(1).broadcast_to((P, E, E))
                z_i = z8[:, :].unsqueeze(2).broadcast_to((P, E, E))
                nc.vector.tensor_tensor(cmp_gt[:, :, :], z_j, z_i, ALU.is_gt)
                gates_c.link(nc.vector.tensor_tensor(cmp_eq[:, :, :], z_j, z_i, ALU.is_equal))
                gates_c.link(nc.vector.tensor_tensor(cmp_eq[:, :, :], cmp_eq[:, :, :], earlier[:, :, :], ALU.mult))
                gates_c.link(nc.vector.tensor_tensor(cmp_gt[:, :, :], cmp_gt[:, :, :], cmp_eq[:, :, :], ALU.add))
                gates_c.link(nc.vector.tensor_reduce(picked[:, :], cmp_gt[:, :, :], AX_X, ALU.add))
                gates_c.link(nc.vector.tensor_scalar(picked[:, :], picked[:, :], 2.0, None, ALU.is_lt))
                after(dve, cnt_tr, t)
                nc.vector.tensor_scalar(cnt[:, 0:E], picked[:, :], CNT_SCALE, None, ALU.mult).then_inc(cnt_ready, 1)
                dve.wait_ge(e8_done, t + 1)
                gates_c.link(nc.vector.tensor_tensor_reduce(out=comb[:, :], in0=picked[:, :], in1=e8[:, :], scale=1.0, scalar=0.0,
                                                            op0=ALU.mult, op1=ALU.add, accum_out=route[:, 2:3]))
                gates_c.link(nc.vector.scalar_tensor_tensor(out=route[:, 3:4], in0=route[:, 1:2], scalar=TOP_EPS, in1=route[:, 2:3],
                                                            op0=ALU.mult, op1=ALU.add))
                gates_c.link(nc.vector.reciprocal(route[:, 4:5], route[:, 3:4]))
                nc.vector.tensor_scalar(comb[:, :], comb[:, :], route[:, 4:5], 1.0 / (H_SCALE * W_SCALE), ALU.mult, ALU.mult).then_inc(comb_ready, 1)
                gates_c.done()

            swi = Chain(dve, swiglu_chain, SWIGLU_STEPS)

            def swiglu(t, w):
                if w == 0:
                    swi.tile(t)
                a, b = f_ps[2 - 2 * w], f_ps[3 - 2 * w]
                dve.wait_ge(tanh_done[w], t + 1)
                swi.link(nc.vector.scalar_tensor_tensor(out=gact[:, :], in0=gact[:, :], scalar=1.0, in1=a, op0=ALU.add, op1=ALU.mult))
                after(dve, hlo_done[1 - w], t + w)
                nc.vector.scalar_tensor_tensor(out=hid[:, :], in0=b, scalar=0.5 * H_SCALE / (X_SCALE * W_SCALE) ** 2, in1=gact[:, :],
                                               op0=ALU.mult, op1=ALU.mult).then_inc(hid_done[w], 1)

            def cnt_copy(t):
                dve.wait_ge(cnt_tr, t + 1)
                nc.vector.tensor_copy(cnt_t[:, :], cnt_ps[0:E + 1, 0:P]).then_inc(cnt_copied, 1)

            def add_shared(t):
                dve.wait_ge(so_mm, t + 1)
                after(dve, out_stored, 16 * t)
                nc.vector.scalar_tensor_tensor(out=acc_o[:, :], in0=f_ps[3][:, 0:C], scalar=1.0 / (H_SCALE * W_SCALE), in1=x1[:, :],
                                               op0=ALU.mult, op1=ALU.add).then_inc(so_used, 1)

            def add_experts(t):
                dve.wait_ge(comb_ready, t + 1)
                dve.wait_ge(so_used, t + 1)
                for p in range(NPAIR):
                    dve.wait_ge(pair_mm, NPAIR * t + p + 1)
                    nc.vector.scalar_tensor_tensor(out=acc_o[:, :], in0=f_ps[p][:, 0:C], scalar=comb[:, 2 * p:2 * p + 1],
                                                   in1=acc_o[:, :], op0=ALU.mult, op1=ALU.add).then_inc(half_added, 1)
                    dve.wait_ge(half_added, NPAIR * t + p + 1)
                    nc.vector.scalar_tensor_tensor(out=acc_o[:, :], in0=f_ps[p][:, C:2 * C], scalar=comb[:, 2 * p + 1:2 * p + 2],
                                                   in1=acc_o[:, :], op0=ALU.mult, op1=ALU.add).then_inc(pair_used, 1)
                    if p < NPAIR - 1:
                        dve.wait_ge(pair_used, NPAIR * t + p + 1)

            def tile(t, attn, ffn, more, last_next=False):
                f = t - 1
                if attn:
                    scores(t, 0)
                    scores(t, 1)
                if not ffn:
                    dve.wait_ge(mean_mm, 1)
                    nc.vector.tensor_scalar(mean_f[:, :, :], mean_ps[:, :].rearrange("p (s c) -> p s c", s=2), 1.0 / N, None,
                                            ALU.mult).then_inc(mean_done, 1)
                if attn:
                    lows(t, 0)
                    if not ffn:
                        dve.wait_ge(mean_done, 2)
                        nc.vector.tensor_tensor(mean_lo[:, :, :], mean_f[:, :, :], mean_hi[:, :, 0:C], ALU.subtract).then_inc(mean_done, 1)
                if ffn:
                    gate(f)
                    swiglu(f, 0)
                if attn:
                    scores(t, 2)
                    lows(t, 1)
                if ffn:
                    cnt_copy(f)
                    swiglu(f, 1)
                    swi.done()
                if attn:
                    lows(t, 2)
                    if more:
                        prepare(t + 1, last_next)
                if ffn:
                    add_shared(f)
                if attn:
                    tail(t)
                if ffn:
                    add_experts(f)

            def v_low(j):
                dve.wait_ge(vh_done, j + 1)
                nc.vector.scalar_tensor_tensor(out=v_lo[:, j, :, :], in0=v_ps[j % 2].rearrange("p (s c) -> p s c", s=2),
                                               scalar=V_SCALE / (X_SCALE * W_SCALE), in1=v_hi[:, j, :, 0:C],
                                               op0=ALU.mult, op1=ALU.subtract).then_inc(vl_done, 1)

            dve.wait_ge(tcols, 3)
            prepare(0)
            for j in range(T):
                v_low(j)
            tile(0, True, False, True)
            for n in range(1, len(weights)):
                weight_lo(n)
            dve.wait_ge(bias_done, 1)
            nc.vector.tensor_scalar(lnsb[:, :, :], lnsb[:, :, :], X_SCALE, None, ALU.mult).then_inc(ln_scaled, 1)
            nc.vector.scalar_tensor_tensor(out=bias_lo[:, :], in0=bias_rows[:, :], scalar=H_SCALE * W_SCALE / CNT_SCALE, in1=bias_hi[:, :],
                                           op0=ALU.mult, op1=ALU.subtract).then_inc(bias_done, 1)
            tile(1, True, True, True)
            with dve.Fori(2, T - 2) as t:
                tile(t, True, True, True)
            tile(T - 2, True, True, True, last_next=True)
            tile(T - 1, True, True, False)
            tile(T, False, True, False)

        @block.tensor
        def _(pe):
            mm = nc.tensor.matmul
            pe.wait_ge(consts, 1)
            for t in range(T):
                pe.wait_ge(inp_ready, t + 1)
                if t >= 2:
                    pe.wait_ge(inp_f, t - 1)
                for k in range(KC):
                    ins = nc.tensor.transpose(tr_ps[t % 2][:, k * P:(k + 1) * P], inp[:, t % 4, k * P:(k + 1) * P], ident_f[:, :])
                ins.then_inc(inp_tr, 1)
            pe.wait_ge(wa_ready, 1)
            pe.wait_ge(inp_f, T)
            for row_ps, s in ((t_ps, 1), (s_ps, 0)):
                for n0 in range(0, NP, 512):
                    n1 = min(n0 + 512, NP)
                    for k in range(KC):
                        ins = mm(row_ps[:, n0:n1], lhsT=wa_rep[:, s, k, :], rhs=inp_t[:, k, n0:n1], start=(k == 0), stop=(k == KC - 1))
                if s == 1:
                    for t in range(T):
                        for k in range(KC):
                            mm(t_ps[:, NP + 2 * t:NP + 2 * t + 2], lhsT=inp_t[:, k, t * P:(t + 1) * P], rhs=wa[:, k, :],
                               start=(k == 0), stop=(k == KC - 1))
            ins.then_inc(st_ready, 1)
            pe.wait_ge(w_lo, 1)
            pe.wait_ge(inp_l, T)
            for j in range(T):
                if j >= 2:
                    pe.wait_ge(vl_done, j - 1)
                terms = [(a, b, k) for k in range(KC) for a, b in ((inp_hi, wt_hi), (inp_hi, wt_lo), (inp_lo, wt_hi))]
                for n, (a, b, k) in enumerate(terms):
                    ins = mm(v_ps[j % 2], lhsT=a[:, k, j * P:(j + 1) * P], rhs=b[:, k:k + KC + 1:KC, :],
                             start=(n == 0), stop=(n == len(terms) - 1))
                ins.then_inc(v_mm, 1)

            pe.wait_ge(tcols, 3)
            for j in range(T):
                ins = nc.tensor.transpose(t_rows_ps[0:6, j * P:(j + 1) * P], t_parts[:, j, :], ident_b[:, :])
            ins.then_inc(t_rows_tr, 1)

            def mrow_part(t):
                pe.wait_ge(mcol_ready, t + 1)
                for s in range(2):
                    ins = nc.tensor.transpose(mrow_ps[0:ROWS, s * P:(s + 1) * P], mcol[:, s, :], ident_b[:, :])
                ins.then_inc(mrow_tr, 1)

            def shifts(t, u):
                j0, n = UNITS[u]
                pe.wait_ge(mrow_ready, t + 1)
                for s in range(2):
                    after(pe, z_done[s], NU * t + u)
                    for j in range(n):
                        o = q_ps[s][:, j * P:(j + 1) * P]
                        mm(o, lhsT=t_rows[:, j0 + j, :], rhs=mrow[0:6, s, :], start=True, stop=False)
                        ins = mm(o, lhsT=madj[:, (j0 + j) * P:(j0 + j + 1) * P], rhs=ident_b[:, :], start=False, stop=True)
                    ins.then_inc(q_ready[s], 1)

            def attend(t, u):
                j0, n = UNITS[u]
                pe.wait_ge(plo_done, NU * t + u + 1)
                if u == 0:
                    after(pe, acc_used, t)
                for s in range(2):
                    for j in range(n):
                        i = slice(j * P, (j + 1) * P)
                        mm(acc_ps[s][:, 0:VW], lhsT=p_hi[:, u, s, i], rhs=v_hi[:, j0 + j, s, 0:VW], start=(j0 + j == 0), stop=False)
                        mm(acc_ps[s][:, 0:C], lhsT=p_hi[:, u, s, i], rhs=v_lo[:, j0 + j, s, :], start=False, stop=False)
                        ins = mm(acc_ps[s][:, 0:VW], lhsT=p_lo[:, u, s, i], rhs=v_hi[:, j0 + j, s, 0:VW], start=False, stop=False)
                    if u == NU - 1:
                        mm(acc_ps[s][:, 0:C], lhsT=mrow[:, s, :], rhs=mean_lo[:, s, :], start=False, stop=False)
                        ins = mm(acc_ps[s][:, 0:VW], lhsT=mrow[:, s, :], rhs=mean_hi[:, s, 0:VW], start=False, stop=True)
                ins.then_inc(att_done, 1)

            def mean_of_v():
                for j in range(T):
                    mm(mean_ps[:, :], lhsT=mean_w[:, :], rhs=v_hi[:, j, :, 0:C], start=(j == 0), stop=False)
                    ins = mm(mean_ps[:, :], lhsT=mean_w[:, :], rhs=v_lo[:, j, :, :], start=False, stop=(j == T - 1))
                ins.then_inc(mean_mm, 1)

            def flat_transposes(t):
                pe.wait_ge(y_ready, t + 1)
                after(pe, pair_used, NPAIR * (t - 1) + 1)
                for k in range(KC):
                    ins = nc.tensor.transpose(f_ps[0][:, k * P:(k + 1) * P], y[:, k * P:(k + 1) * P], ident_f[:, :])
                ins.then_inc(flat_tr, 1)

            def gate_logits(t):
                pe.wait_ge(flat_f, KC * (t + 1))
                after(pe, pair_used, NPAIR * (t - 1) + 2)
                for k in range(KC):
                    ins = mm(f_ps[1][:, 0:G + E], lhsT=flat[:, k, :], rhs=gates[:, k, :], start=(k == 0), stop=(k == KC - 1))
                ins.then_inc(logits, 1)

            def hidden(t, w):
                pe.wait_ge(flat_l, t + 1)
                for half in range(2):
                    if w == 0:
                        after(pe, pair_used, NPAIR * (t - 1) + 3 + half)
                    elif half == 1:
                        pe.wait_ge(gl_done, t + 1)
                    bank = f_ps[2 - 2 * w + half]
                    for c in range(KH):
                        cols = slice(half * H + c * P, half * H + (c + 1) * P)
                        terms = [(a, b, k) for k in range(KC) for a, b in ((in_hi, flat_hi), (in_hi, flat_lo), (in_lo, flat_hi))]
                        for n, (a, b, k) in enumerate(terms):
                            ins = mm(bank[:, c * P:(c + 1) * P], lhsT=a[:, w, k, cols], rhs=b[:, k, :], start=(n == 0), stop=(n == len(terms) - 1))
                ins.then_inc(in_mm[w], 1)

            def counts(t):
                pe.wait_ge(cnt_ready, t + 1)
                pe.wait_ge(hid_done[0], t + 1)
                nc.tensor.transpose(cnt_ps[0:E + 1, 0:P], cnt[:, 0:E + 1], ident_h[:, :]).then_inc(cnt_tr, 1)

            def shared_out(t):
                pe.wait_ge(hlo_done[0], t + 1)
                pe.wait_ge(cnt_copied, t + 1)
                o = f_ps[3][:, 0:C]
                for k in range(KH):
                    mm(o, lhsT=h_hi[:, 0, k, :], rhs=so_hi[:, k, :], start=(k == 0), stop=False)
                    mm(o, lhsT=h_hi[:, 0, k, :], rhs=so_lo[:, k, :], start=False, stop=False)
                    mm(o, lhsT=h_lo[:, 0, k, :], rhs=so_hi[:, k, :], start=False, stop=False)
                mm(o, lhsT=cnt_t[:, :], rhs=bias_lo[:, :], start=False, stop=False)
                mm(o, lhsT=cnt_t[:, :], rhs=bias_hi[:, :], start=False, stop=True).then_inc(so_mm, 1)

            def expert_pair(t, p):
                pe.wait_ge(hlo_done[1], t + 1)
                if p == 2:
                    pe.wait_ge(cnt_copied, t + 1)
                if p == 3:
                    pe.wait_ge(so_used, t + 1)
                cols = slice(2 * p * C, (2 * p + 2) * C)
                for k in range(KH):
                    mm(f_ps[p], lhsT=h_hi[:, 1, k, :], rhs=ew[:, 0, k, cols], start=(k == 0), stop=False)
                    mm(f_ps[p], lhsT=h_hi[:, 1, k, :], rhs=ew[:, 1, k, cols], start=False, stop=False)
                    ins = mm(f_ps[p], lhsT=h_lo[:, 1, k, :], rhs=ew[:, 0, k, cols], start=False, stop=(k == KH - 1))
                ins.then_inc(pair_mm, 1)

            def tile(t, attn, ffn, more):
                f = t - 1
                if attn:
                    shifts(t, 0)
                if ffn:
                    flat_transposes(f)
                if attn:
                    shifts(t, 1)
                if not ffn:
                    pe.wait_ge(t_rows_done, 1)
                    mean_of_v()
                if ffn:
                    gate_logits(f)
                    hidden(f, 0)
                if attn:
                    attend(t, 0)
                    shifts(t, 2)
                if ffn:
                    hidden(f, 1)
                if attn:
                    attend(t, 1)
                if ffn:
                    counts(f)
                    shared_out(f)
                if attn:
                    if not ffn:
                        pe.wait_ge(mean_done, 3)
                    attend(t, 2)
                if ffn:
                    expert_pair(f, 0)
                if more:
                    mrow_part(t + 1)
                if ffn:
                    if more:
                        pe.wait_ge(mrow_ready, t + 2)
                    for p in range(1, NPAIR):
                        expert_pair(f, p)

            mrow_part(0)
            pe.wait_ge(vl_done, T)
            pe.wait_ge(ramp_ready, T)
            pe.wait_ge(t_rows_done, 1)
            tile(0, True, False, True)
            pe.wait_ge(w_lo, len(weights))
            pe.wait_ge(bias_done, 2)
            pe.wait_ge(small_in, 7 * 16)
            tile(1, True, True, True)
            with pe.Fori(2, T - 1) as t:
                tile(t, True, True, True)
            tile(T - 1, True, True, False)
            tile(T, False, True, False)


def kernel(**inputs):
    import numpy as np
    import concourse.bacc as bacc
    from concourse.bass_utils import run_bass_kernel_spmd

    def arr(name):
        return np.asarray(inputs[name])

    laid = {
        "x": arr("x"),
        "adj": arr("adj"),
        "gat_w": arr("L0_gnn_W"),
        "gat_a": arr("L0_gnn_a").reshape(2, -1),
        "wtrans": arr("L0_gnn_wtrans"),
        "ln_pair": np.stack([arr("L0_ffn_ln_scale"), arr("L0_ffn_ln_bias")]).reshape(2, -1, P).transpose(2, 0, 1),
        "sh_in": arr("L0_ffn_shared_in_w").T,
        "sh_out": arr("L0_ffn_shared_out_w").T,
        "sh_out_b": arr("L0_ffn_shared_out_b"),
        "ex_in": arr("L0_ffn_expert_in_w").T,
        "ex_out": arr("L0_ffn_expert_out_weight").transpose(2, 0, 1),
        "ex_out_b": arr("L0_ffn_expert_out_bias"),
        "group_gate": arr("L0_ffn_group_gate_w").T,
        "expert_gate": arr("L0_ffn_expert_gate_w").T,
        "group_bias": arr("L0_ffn_group_bias"),
        "expert_bias": arr("L0_ffn_expert_bias"),
    }
    nc = bacc.Bacc("TRN2", target_bir_lowering=False, num_devices=1)
    arrays, args = {}, []
    for name, a in laid.items():
        arrays[name] = np.ascontiguousarray(a)
        args.append(nc.dram_tensor(name, a.shape, mybir.dt.from_np(a.dtype), kind="ExternalInput").ap())
    out = nc.dram_tensor("out", laid["x"].shape, F32, kind="ExternalOutput").ap()
    gnn_moe_kernel(nc, *args, out)
    r = run_bass_kernel_spmd(nc, [arrays], core_ids=[0])
    return r.results[0]["out"]
```

```python
from contextlib import ExitStack

import concourse.bass as bass
from concourse import mybir

P = 128
F32 = mybir.dt.float32
F16 = mybir.dt.float16
BF16 = mybir.dt.bfloat16
ALU = mybir.AluOpType
ACT = mybir.ActivationFunctionType
AX_X = mybir.AxisListType.X

BIG = 1e30
NO_NEIGHBOUR = -1e29
SLOPE = 0.2
EPS = 1e-5
TOP_EPS = 1e-8
X_SCALE = 2.0 ** 5
W_SCALE = 2.0 ** 8
V_SCALE = 2.0 ** 6
P_LOG_SCALE = 9.010913347279288
H_SCALE = 2.0 ** 4
CNT_SCALE = 2.0 ** 6

PREP_STEPS = 9
TAIL_STEPS = 7
GATE_STEPS = 10
SWIGLU_STEPS = 2


def gnn_moe_kernel(nc, x, adj, gat_w, gat_a, wtrans, ln_pair, sh_in, sh_out, sh_out_b,
                   ex_in, ex_out, ex_out_b, group_gate, expert_gate, group_bias, expert_bias, out):
    N, C = x.shape
    T = -(-N // P)
    NP = T * P
    LAST = N - (T - 1) * P
    KC = C // P
    H = sh_out.shape[0]
    KH = H // P
    E = ex_out.shape[1]
    G = group_gate.shape[1]
    EG = E // G
    VW = C + 1
    ROWS = 7
    UNITS = [(0, 4), (4, 4), (8, T - 8)]
    NU = len(UNITS)
    STAGES = 6
    PAIR_BANK = [0, 2, 3, 1]
    NPAIR = E // 2
    TAIL = [((T - 1) * P, 0, 64), ((T - 1) * P + 64, 64, LAST - 64)]
    assert C == 256 and KH == 4 and E == 8 and T == 11 and LAST > 64

    with ExitStack() as ctx:
        def sb(name, shape, dt=F32):
            return ctx.enter_context(nc.sbuf_tensor(name, shape, dt))

        def sem(name):
            return ctx.enter_context(nc.semaphore(name))

        xall = sb("xall", [P, T, C])
        ramp = sb("ramp", [P, T, P])
        s_row = sb("s_row", [P, NP])
        v_hi = sb("v_hi", [P, T, 2, VW + 1], F16)
        v_lo = sb("v_lo", [P, T, 2, C], F16)
        t_row = sb("t_row", [P, NP])
        st_col = sb("st_col", [P, T, 2])
        in_hi = sb("in_hi", [P, 2, KC, 2 * H], F16)
        in_lo = sb("in_lo", [P, 2, KC, 2 * H], F16)
        so_hi = sb("so_hi", [P, KH, C], F16)
        so_lo = sb("so_lo", [P, KH, C], F16)
        ew = sb("ew", [P, 2, KH, E * C], F16)
        gates = sb("gates", [P, KC, G + E])
        gate_bias = sb("gate_bias", [P, G + E])
        lnsb = sb("lnsb", [P, 2, KC])
        bias_rows = sb("bias_rows", [E + 1, C])
        bias_hi = sb("bias_hi", [E + 1, C], F16)
        bias_lo = sb("bias_lo", [E + 1, C], F16)
        mean_hi = sb("mean_hi", [ROWS, 2, VW + 1], F16)
        mean_lo = sb("mean_lo", [ROWS, 2, C], F16)
        mean_w = sb("mean_w", [P, ROWS], F16)
        ident_b = sb("ident_b", [P, P], BF16)
        ident_h = sb("ident_h", [P, P], F16)
        ident_f = sb("ident_f", [P, P])
        t_parts = sb("t_parts", [P, T, 6], BF16)
        t_rows = sb("t_rows", [6, T, P], BF16)
        t_ramp = sb("t_ramp", [P, T])
        slope_s = sb("slope_s", [P, T])
        one_col = sb("one_col", [P, 1])
        neg_half = sb("neg_half", [P, T])
        signs = sb("signs", [P, 2])
        unscale = sb("unscale", [P, 2])
        earlier = sb("earlier", [P, E, E])
        adj_sb = sb("adj_sb", [P, N])
        madj = sb("madj", [P, NP], BF16)
        ttr_out = sb("ttr_out", [P, N], BF16)
        stat = sb("stat", [P, 16])
        mcol = sb("mcol", [P, 2, ROWS], BF16)
        mrow = sb("mrow", [ROWS, 2, P], BF16)
        prob_size, part_size = 2 * 2 * 4 * P, NU * 2 * 4 * P
        work = sb("work", [P, prob_size + part_size])
        prob = work[:, 0:prob_size].rearrange("p (b s n) -> p b s n", b=2, s=2)
        p_parts = work[:, prob_size:prob_size + part_size].bitcast(F16)
        p_hi, p_lo = (p_parts[:, h * part_size:(h + 1) * part_size].rearrange("p (u s n) -> p u s n", u=NU, s=2)
                      for h in range(2))
        tail_sb = sb("tail_sb", [P, 4, C])
        new, elu, x1, y = (tail_sb[:, n, :] for n in range(4))
        bn = sb("bn", [P, 6])
        mv = sb("mv", [P, 4])
        carrier = sb("carrier", [1, 1])
        flat = sb("flat", [P, KC, P])
        flat_hi = sb("flat_hi", [P, KC, P], F16)
        flat_lo = sb("flat_lo", [P, KC, P], F16)
        gl = sb("gl", [P, G + E])
        pen = sb("pen", [P, G])
        z8 = sb("z8", [P, E])
        cmp_gt = sb("cmp_gt", [P, E, E])
        cmp_eq = sb("cmp_eq", [P, E, E])
        route = sb("route", [P, 8])
        e8 = sb("e8", [P, E])
        picked = sb("picked", [P, E])
        comb = sb("comb", [P, E])
        cnt = sb("cnt", [P, E + 2], F16)
        cnt_t = sb("cnt_t", [E + 1, P], F16)
        gact = sb("gact", [P, KH * P])
        hid = sb("hid", [P, KH * P])
        h_hi = sb("h_hi", [P, 2, KH, P], F16)
        h_lo = sb("h_lo", [P, 2, KH, P], F16)
        acc_o = sb("acc_o", [P, C])
        stage = sb("stage", [P, STAGES, 1024])
        words = [0]

        def early(n):
            words[0] += n
            return work[:, words[0] - n:words[0]]

        inp = early(T * C).rearrange("p (t c) -> p t c", c=C)
        inp_hi = sb("inp_hi", [P, KC, NP], F16)
        inp_lo = sb("inp_lo", [P, KC, NP], F16)
        wt_hi = sb("wt_hi", [P, 2 * KC, C], F16)
        wt_lo = sb("wt_lo", [P, 2 * KC, C], F16)
        gw_sb = early(KC * C).rearrange("p (k c) -> p k c", c=C)
        ga_sb = early(2 * C).rearrange("p (k c) -> p k c", c=C)
        wa_out = early(C)
        wa = sb("wa", [P, KC, 2])
        wa_parts = sb("wa_parts", [P, 2, KC, 2], F16)
        wa_rep = sb("wa_rep", [P, 2, KC, 2, P], F16)
        bn0 = sb("bn0", [P, T, 6])
        mv0 = sb("mv0", [P, T, 2])
        rs0 = sb("rs0", [P, T])
        norm0 = sb("norm0", [P, 2, T])
        t_rest = sb("t_rest", [P, 2, T])
        mean_f = sb("mean_f", [ROWS, 2, C])

        psum = ctx.enter_context(nc.psum_tensor("psum", [P, 8, 512], F32))
        q_ps = [psum[:, 0, :], psum[:, 1, :]]
        acc_ps = [psum[:, 2, :], psum[:, 3, :]]
        f_ps = [psum[:, 4 + i, :] for i in range(4)]
        s_ps = psum[:, 2:5, :].rearrange("p b n -> p (b n)")
        t_ps = psum[:, 5:8, :].rearrange("p b n -> p (b n)")
        tr_ps = [psum[:, n, 0:KC * P] for n in range(2)]
        v_ps = [psum[:, 0, :], psum[:, 1, :]]
        mean_ps = psum[0:ROWS, 6, :]
        mrow_ps = f_ps[1].bitcast(BF16)
        t_rows_ps = psum[:, 6:8, :].rearrange("p b n -> p (b n)").bitcast(BF16)
        logit_ps = f_ps[0][:, C:C + G + E]
        cnt_ps = f_ps[2].bitcast(F16)

        x_in = [sem(f"x_in{i}") for i in range(3)]
        gat_in = sem("gat_in")
        small_in = sem("small_in")
        staged = [sem(f"staged{n}") for n in range(STAGES)]
        x_pad = sem("x_pad")
        consts = sem("consts")
        pool_chain = sem("pool_chain")
        stats0 = sem("stats0")
        rstd0 = sem("rstd0")
        start_chain = sem("start_chain")
        wa_ready = sem("wa_ready")
        inp_ready = sem("inp_ready")
        inp_tr = sem("inp_tr")
        inp_h = sem("inp_h")
        normed0 = sem("normed0")
        rows_done = sem("rows_done")
        inp_l = sem("inp_l")
        st_ready = sem("st_ready")
        st_cols_ready = sem("st_cols_ready")
        tcols = sem("tcols")
        ramp_ready = sem("ramp_ready")
        v_mm = sem("v_mm")
        vh_done = sem("vh_done")
        vl_done = sem("vl_done")
        t_rows_tr = sem("t_rows_tr")
        t_rows_done = sem("t_rows_done")
        mean_mm = sem("mean_mm")
        mean_done = sem("mean_done")
        w_hi = sem("w_hi")
        w_lo = sem("w_lo")
        w_lo_pool = sem("w_lo_pool")
        w_scaled = sem("w_scaled")
        bias_done = sem("bias_done")
        ln_scaled = sem("ln_scaled")
        adj_in = sem("adj_in")
        madj_ready = sem("madj_ready")
        prep_chain = sem("prep_chain")
        mcol_ready = sem("mcol_ready")
        mrow_tr = sem("mrow_tr")
        mrow_ready = sem("mrow_ready")
        q_ready = [sem("q_ready0"), sem("q_ready1")]
        z_done = [sem("z_done0"), sem("z_done1")]
        exp_done = sem("exp_done")
        phi_done = sem("phi_done")
        plo_done = sem("plo_done")
        att_done = sem("att_done")
        tail_chain = sem("tail_chain")
        acc_used = sem("acc_used")
        new_neg = sem("new_neg")
        elu_exp = sem("elu_exp")
        stats1 = sem("stats1")
        rstd1 = sem("rstd1")
        y_ready = sem("y_ready")
        flat_tr = sem("flat_tr")
        flat_f = sem("flat_f")
        flat_h = sem("flat_h")
        flat_l = sem("flat_l")
        logits = sem("logits")
        gl_done = sem("gl_done")
        gate_chain = sem("gate_chain")
        swiglu_chain = sem("swiglu_chain")
        negmax = sem("negmax")
        e8_done = sem("e8_done")
        cnt_ready = sem("cnt_ready")
        cnt_tr = sem("cnt_tr")
        cnt_copied = sem("cnt_copied")
        in_mm = [sem("in_mm_shared"), sem("in_mm_expert")]
        tanh_done = [sem("tanh_shared"), sem("tanh_expert")]
        hid_done = [sem("hid_shared"), sem("hid_expert")]
        hhi_done = [sem("hhi_shared"), sem("hhi_expert")]
        hlo_done = [sem("hlo_shared"), sem("hlo_expert")]
        so_mm = sem("so_mm")
        so_used = sem("so_used")
        comb_ready = sem("comb_ready")
        half_added = sem("half_added")
        pair_mm = sem("pair_mm")
        pair_used = sem("pair_used")
        out_stored = sem("out_stored")

        def after(eng, s, n):
            if not isinstance(n, int) or n > 0:
                eng.wait_ge(s, n)

        def hold():
            nc.vector.memset(carrier[:, :], 0.0)

        class Chain:
            def __init__(self, eng, s, per_tile):
                self.eng, self.s, self.per_tile = eng, s, per_tile

            def tile(self, t):
                self.t, self.k = t, 0

            def link(self, ins):
                self.k += 1
                ins.then_inc(self.s, 1)
                self.eng.wait_ge(self.s, self.t * self.per_tile + self.k)

            def done(self):
                assert self.k == self.per_tile, (self.s, self.k)

        def weight_list():
            lst = [(wtrans.rearrange("(b p) c -> p b c", p=P), wt_hi, wt_lo)]
            for w, src in ((0, sh_in), (1, ex_in)):
                for k in range(KC):
                    lst.append((src[k * P:(k + 1) * P, :], in_hi[:, w, k, :], in_lo[:, w, k, :]))
            lst.append((sh_out.rearrange("(k p) c -> p k c", p=P), so_hi[:, :, :], so_lo[:, :, :]))
            for k in range(KH):
                for half in range(2):
                    e = slice(half * E // 2, (half + 1) * E // 2)
                    c = slice(half * E // 2 * C, (half + 1) * E // 2 * C)
                    lst.append((ex_out[k * P:(k + 1) * P, e, :], ew[:, 0, k, c], ew[:, 1, k, c]))
            return lst

        weights = weight_list()
        BY_POOL = (4, 6, 8, 10, 12)

        def low_done(eng, n):
            if n in BY_POOL:
                eng.wait_ge(w_lo_pool, BY_POOL.index(n) + 1)
            else:
                eng.wait_ge(w_lo, n + 1 - sum(m < n for m in BY_POOL))

        def stage_view(n, like):
            v = stage[:, n % STAGES, :]
            if len(like.shape) == 2:
                return v
            return v.rearrange("p (a b) -> p a b", b=like.shape[2])

        def flat_free(ap):
            return ap if len(ap.shape) == 2 else ap.rearrange("p a b -> p (a b)")

        block = ctx.enter_context(nc.Block())

        @block.sync
        def _(sp):
            sp.dma_start(xall[:, 0:4, :], x[0:4 * P, :].rearrange("(t p) c -> p t c", p=P)).then_inc(x_in[0], 16)
            sp.dma_start(xall[:, 4:T - 1, :], x[4 * P:(T - 1) * P, :].rearrange("(t p) c -> p t c", p=P)).then_inc(x_in[1], 16)
            sp.wait_ge(x_pad, 1)
            for row, part, n in TAIL:
                sp.dma_start(xall[part:part + n, T - 1, :], x[row:row + n, :]).then_inc(x_in[2], 16)

            def load_weight(n):
                src = weights[n][0]
                if n >= STAGES:
                    low_done(sp, n - STAGES)
                sp.dma_start(stage_view(n, src), src).then_inc(staged[n % STAGES], 16)

            sp.dma_start(gw_sb[:, :, :], gat_w.rearrange("(k p) c -> p k c", p=P)).then_inc(gat_in, 16)
            sp.dma_start(ga_sb[:, :, :], gat_a.partition_broadcast(P)).then_inc(gat_in, 16)
            load_weight(0)
            sp.dma_start(adj_sb[:, :], adj[0:P, :]).then_inc(adj_in, 16)
            for n in range(1, STAGES):
                load_weight(n)
            sp.dma_start(gates[:, :, 0:G], group_gate.rearrange("(k p) g -> p k g", p=P)).then_inc(small_in, 16)
            sp.dma_start(gates[:, :, G:G + E], expert_gate.rearrange("(k p) g -> p k g", p=P)).then_inc(small_in, 16)
            sp.dma_start(gate_bias[:, 0:G], group_bias.partition_broadcast(P)).then_inc(small_in, 16)
            sp.dma_start(gate_bias[:, G:G + E], expert_bias.partition_broadcast(P)).then_inc(small_in, 16)
            sp.dma_start(lnsb[:, :, :], ln_pair).then_inc(small_in, 16)
            sp.dma_start(bias_rows[0:E, :], ex_out_b).then_inc(small_in, 16)
            sp.dma_start(bias_rows[E:E + 1, :], sh_out_b.rearrange("(o c) -> o c", o=1)).then_inc(small_in, 16)
            for n in range(STAGES, len(weights)):
                load_weight(n)
            sp.wait_ge(madj_ready, 1)
            sp.dma_start(adj_sb[:, :], adj[P:2 * P, :]).then_inc(adj_in, 16)

            def store(t, row, part, n):
                sp.wait_ge(pair_used, NPAIR * (t + 1))
                sp.dma_start(out[row:row + n, :] if isinstance(row, int) else out[bass.ds(row, n), :],
                             acc_o[part:part + n, :]).then_inc(out_stored, 16)

            sp.wait_ge(madj_ready, 2)
            sp.dma_start(adj_sb[:, :], adj[2 * P:3 * P, :]).then_inc(adj_in, 16)
            with sp.Fori(2, T - 2) as t:
                sp.wait_ge(madj_ready, t + 1)
                sp.dma_start(adj_sb[:, :], adj[bass.ds((t + 1) * P, P), :]).then_inc(adj_in, 16)
                store(t - 2, (t - 2) * P, 0, P)
            sp.wait_ge(madj_ready, T - 1)
            for row, part, n in TAIL:
                sp.dma_start(adj_sb[part:part + n, :], adj[row:row + n, :]).then_inc(adj_in, 16)
            for t in range(T - 4, T - 1):
                store(t, t * P, 0, P)
            for row, part, n in TAIL:
                store(T - 1, row, part, n)
            sp.wait_ge(out_stored, 16 * (T + 1))

        @block.gpsimd
        def _(pool):
            nc.gpsimd.memset(xall[:, T - 1, :], 0.0).then_inc(x_pad, 1)
            steps = [0]

            def link(ins):
                steps[0] += 1
                ins.then_inc(pool_chain, 1)
                pool.wait_ge(pool_chain, steps[0])

            nc.gpsimd.memset(ident_b[:, :], 0.0)
            nc.gpsimd.memset(ident_h[:, :], 0.0)
            nc.gpsimd.memset(mean_w[:, :], 0.0)
            nc.gpsimd.memset(neg_half[:, :], -0.5)
            link(nc.gpsimd.memset(ident_f[:, :], 0.0))
            for m in (ident_f, ident_b, ident_h):
                nc.gpsimd.affine_select(out=m[:, :], in_=m[:, :], compare_op=ALU.not_equal, fill=1.0, base=0,
                                        pattern=[[-1, P]], channel_multiplier=1)
            nc.gpsimd.memset(mean_w[:, ROWS - 1:ROWS], 1.0)
            nc.gpsimd.memset(t_parts[:, :, 0:3], 1.0)
            nc.gpsimd.memset(mcol[:, 0, 3:6], 1.0)
            nc.gpsimd.memset(mcol[:, 1, 3:6], -1.0)
            nc.gpsimd.memset(one_col[:, :], 1.0)
            nc.gpsimd.memset(signs[:, 0:1], -1.0)
            nc.gpsimd.memset(signs[:, 1:2], 1.0)
            nc.gpsimd.memset(unscale[:, 0:1], 1.0 / V_SCALE)
            nc.gpsimd.memset(unscale[:, 1:2], -1.0 / V_SCALE)
            nc.gpsimd.memset(cnt[:, :], CNT_SCALE)
            nc.gpsimd.memset(mean_hi[:, :, :], 0.0)
            nc.gpsimd.memset(v_hi[:, :, :, C:VW + 1], 1.0)
            nc.gpsimd.memset(madj[:, N:NP], -BIG)
            nc.gpsimd.memset(t_row[:, N:NP], 0.0)
            link(nc.gpsimd.memset(earlier[:, :, :], 1.0))
            nc.gpsimd.affine_select(out=earlier[:, :, :], in_=earlier[:, :, :], compare_op=ALU.is_gt, fill=0.0,
                                    base=0, pattern=[[1, E], [-1, E]], channel_multiplier=0).then_inc(consts, 1)
            for a, b in ((0, 4), (4, T)):
                pool.wait_ge(stats0, b)
                link(nc.gpsimd.tensor_scalar(rs0[:, a:b], mv0[:, a:b, 1], EPS, None, ALU.add))
                nc.gpsimd.tensor_tensor(rs0[:, a:b], rs0[:, a:b], neg_half[:, a:b], ALU.pow).then_inc(rstd0, 1)
            def rstd(t):
                pool.wait_ge(stats1, t + 1)
                nc.gpsimd.tensor_tensor(mv[:, 3:4], mv[:, 2:3], neg_half[:, 0:1], ALU.pow).then_inc(rstd1, 1)

            def weight_lo(n):
                _, hi, lo = weights[n]
                k = BY_POOL.index(n) + 1
                pool.wait_ge(w_hi, n + 1)
                st = stage[:, n % STAGES, :]
                nc.gpsimd.tensor_scalar(st, st, W_SCALE, 1.0, ALU.mult, ALU.mult).then_inc(w_scaled, 1)
                pool.wait_ge(w_scaled, k)
                nc.gpsimd.tensor_tensor(flat_free(lo), st, flat_free(hi), ALU.subtract).then_inc(w_lo_pool, 1)

            def lows(t, u):
                w = UNITS[u][1] * P
                pool.wait_ge(phi_done, NU * t + u + 1)
                nc.gpsimd.tensor_tensor(p_lo[:, u, :, 0:w], prob[:, u % 2, :, 0:w], p_hi[:, u, :, 0:w], ALU.subtract).then_inc(plo_done, 1)

            def flat_low(t):
                pool.wait_ge(flat_h, t + 1)
                nc.gpsimd.tensor_tensor(flat_lo[:, :, :], flat[:, :, :], flat_hi[:, :, :], ALU.subtract).then_inc(flat_l, 1)

            def hid_low(t, w):
                pool.wait_ge(hhi_done[w], t + 1)
                nc.gpsimd.tensor_tensor(h_lo[:, w, :, :], hid[:, :].rearrange("p (k n) -> p k n", k=KH),
                                        h_hi[:, w, :, :], ALU.subtract).then_inc(hlo_done[w], 1)

            def tile(t, attn, ffn):
                f = t - 1
                if ffn:
                    flat_low(f)
                if attn:
                    lows(t, 0)
                    lows(t, 1)
                if ffn:
                    hid_low(f, 0)
                if attn:
                    lows(t, 2)
                if ffn:
                    hid_low(f, 1)
                if attn:
                    rstd(t)

            for n in BY_POOL:
                weight_lo(n)
            tile(0, True, False)
            tile(1, True, True)
            with pool.Fori(2, T) as t:
                tile(t, True, True)
            tile(T, False, True)

        @block.scalar
        def _(act):
            def weight_hi(n):
                src, hi, _ = weights[n]
                act.wait_ge(staged[n % STAGES], 16 * (n // STAGES + 1))
                nc.scalar.activation(flat_free(hi), stage[:, n % STAGES, :], ACT.Copy, scale=W_SCALE).then_inc(w_hi, 1)

            def normalise(t):
                act.wait_ge(normed0, t + 1)
                nc.scalar.activation(inp[:, t, :], xall[:, t, :], ACT.Identity, bias=norm0[:, 1, t:t + 1],
                                     scale=norm0[:, 0, t:t + 1]).then_inc(inp_ready, 1)

            def inp_high(t):
                act.wait_ge(inp_tr, t + 1)
                nc.scalar.activation(inp_hi[:, :, t * P:(t + 1) * P], tr_ps[t % 2].rearrange("p (k n) -> p k n", k=KC),
                                     ACT.Copy).then_inc(inp_h, 1)

            for t in range(T):
                normalise(t)
                if t >= 1:
                    inp_high(t - 1)
                if t == 6:
                    weight_hi(0)
            inp_high(T - 1)
            weight_hi(1)
            weight_hi(2)
            act.wait_ge(st_ready, 1)
            nc.scalar.activation(t_row[:, 0:N], t_ps[:, 0:N], ACT.Copy, scale=1.0 / (X_SCALE * W_SCALE)).then_inc(rows_done, 1)
            nc.scalar.activation(s_row[:, :], s_ps[:, 0:NP], ACT.Copy, scale=1.0 / (X_SCALE * W_SCALE)).then_inc(rows_done, 1)
            n = 3
            for j in range(T):
                act.wait_ge(v_mm, j + 1)
                nc.scalar.activation(v_hi[:, j, :, 0:C], v_ps[j % 2].rearrange("p (s c) -> p s c", s=2), ACT.Copy,
                                     scale=V_SCALE / (X_SCALE * W_SCALE)).then_inc(vh_done, 1)
                if n < len(weights):
                    weight_hi(n)
                    n += 1
            while n < len(weights):
                weight_hi(n)
                n += 1

            def ramps(t):
                i = slice(t * P, (t + 1) * P) if isinstance(t, int) else bass.ds(t * P, P)
                for j in range(T):
                    nc.scalar.activation(ramp[:, j, :], s_row[:, i], ACT.Relu, bias=t_ramp[:, j:j + 1], scale=1.0 - SLOPE).then_inc(ramp_ready, 1)

            def exps(t, u):
                w = UNITS[u][1] * P
                for s in range(2):
                    act.wait_ge(z_done[s], NU * t + u + 1)
                pr = prob[:, u % 2, :, 0:w]
                nc.scalar.activation(pr, pr, ACT.Exp).then_inc(exp_done, 1)

            def highs(t, u):
                w = UNITS[u][1] * P
                act.wait_ge(exp_done, NU * t + u + 1)
                after(act, att_done, NU * (t - 1) + u + 1)
                nc.scalar.activation(p_hi[:, u, :, 0:w], prob[:, u % 2, :, 0:w], ACT.Copy).then_inc(phi_done, 1)

            def mrow_copy(t):
                act.wait_ge(mrow_tr, t + 1)
                nc.scalar.activation(mrow[:, :, :], mrow_ps[0:ROWS, 0:2 * P].rearrange("p (s n) -> p s n", s=2), ACT.Copy).then_inc(mrow_ready, 1)

            def elu_part(t):
                act.wait_ge(new_neg, t + 1)
                nc.scalar.activation(elu[:, :], elu[:, :], ACT.Exp).then_inc(elu_exp, 1)

            def flat_part(t):
                act.wait_ge(flat_tr, t + 1)
                ps = f_ps[0][:, 0:KC * P].rearrange("p (k n) -> p k n", k=KC)
                after(act, flat_l, t)
                for k in range(KC):
                    nc.scalar.activation(flat[:, k, :], ps[:, k, :], ACT.Identity, bias=lnsb[:, 1, k:k + 1],
                                         scale=lnsb[:, 0, k:k + 1]).then_inc(flat_f, 1)
                act.wait_ge(flat_f, KC * (t + 1))
                nc.scalar.activation(flat_hi[:, :, :], flat[:, :, :], ACT.Copy).then_inc(flat_h, 1)

            def tanhs(t, w):
                act.wait_ge(in_mm[w], t + 1)
                nc.scalar.activation(gact[:, :], f_ps[2 - 2 * w], ACT.Tanh, scale=0.5 / (X_SCALE * W_SCALE)).then_inc(tanh_done[w], 1)

            def hid_high(t, w):
                act.wait_ge(hid_done[w], t + 1)
                after(act, *((so_mm, t) if w == 0 else (pair_mm, NPAIR * t)))
                nc.scalar.activation(h_hi[:, w, :, :], hid[:, :].rearrange("p (k n) -> p k n", k=KH), ACT.Copy).then_inc(hhi_done[w], 1)

            def route_exp(t):
                act.wait_ge(negmax, t + 1)
                nc.scalar.activation(e8[:, :], z8[:, :], ACT.Exp, bias=route[:, 0:1], accum_out=route[:, 1:2]).then_inc(e8_done, 1)

            def cnt_copy(t):
                act.wait_ge(cnt_tr, t + 1)
                nc.scalar.activation(cnt_t[:, :], cnt_ps[0:E + 1, 0:P], ACT.Copy).then_inc(cnt_copied, 1)

            def tile(t, attn, ffn, more):
                f = t - 1
                if ffn:
                    flat_part(f)
                if attn:
                    exps(t, 0)
                    highs(t, 0)
                    exps(t, 1)
                    highs(t, 1)
                if not ffn:
                    act.wait_ge(mean_done, 1)
                    nc.scalar.activation(mean_hi[:, :, 0:C], mean_f[:, :, :], ACT.Copy).then_inc(mean_done, 1)
                if ffn:
                    route_exp(f)
                    tanhs(f, 0)
                    hid_high(f, 0)
                if attn:
                    exps(t, 2)
                    highs(t, 2)
                if ffn:
                    tanhs(f, 1)
                    cnt_copy(f)
                    hid_high(f, 1)
                if more:
                    ramps(t + 1)
                    mrow_copy(t + 1)
                if attn:
                    elu_part(t)

            act.wait_ge(tcols, 2)
            act.wait_ge(rows_done, 2)
            ramps(0)
            act.wait_ge(t_rows_tr, 1)
            nc.scalar.activation(t_rows[:, :, :], t_rows_ps[0:6, 0:NP].rearrange("p (t n) -> p t n", n=P), ACT.Copy).then_inc(t_rows_done, 1)
            mrow_copy(0)
            act.wait_ge(small_in, 7 * 16)
            nc.scalar.activation(bias_hi[:, :], bias_rows[:, :], ACT.Copy, scale=H_SCALE * W_SCALE / CNT_SCALE).then_inc(bias_done, 1)
            tile(0, True, False, True)
            act.wait_ge(ln_scaled, 1)
            tile(1, True, True, True)
            with act.Fori(2, T - 1) as t:
                tile(t, True, True, True)
            tile(T - 1, True, True, False)
            tile(T, False, True, False)

        @block.vector
        def _(dve):
            steps = [0]

            def link(ins):
                steps[0] += 1
                ins.then_inc(start_chain, 1)
                dve.wait_ge(start_chain, steps[0])

            def weight_lo(n):
                _, hi, lo = weights[n]
                dve.wait_ge(w_hi, n + 1)
                nc.vector.scalar_tensor_tensor(out=flat_free(lo), in0=stage[:, n % STAGES, :], scalar=W_SCALE, in1=flat_free(hi),
                                               op0=ALU.mult, op1=ALU.subtract).then_inc(w_lo, 1)

            def statistics(a, b):
                for t in range(a, b):
                    link(nc.vector.bn_stats(bn0[:, t, :], xall[:, t, :]))
                    nc.vector.bn_aggr(mv0[:, t, :], bn0[:, t, :]).then_inc(stats0, 1)

            def norms(part, a, b):
                dve.wait_ge(rstd0, part + 1)
                link(nc.vector.tensor_scalar(norm0[:, 0, a:b], rs0[:, a:b], X_SCALE, None, ALU.mult))
                nc.vector.scalar_tensor_tensor(out=norm0[:, 1, a:b], in0=mv0[:, a:b, 0], scalar=-1.0, in1=norm0[:, 0, a:b],
                                               op0=ALU.mult, op1=ALU.mult).then_inc(normed0, b - a)

            def inp_low(t):
                dve.wait_ge(inp_h, t + 1)
                nc.vector.tensor_tensor(inp_lo[:, :, t * P:(t + 1) * P], tr_ps[t % 2].rearrange("p (k n) -> p k n", k=KC),
                                        inp_hi[:, :, t * P:(t + 1) * P], ALU.subtract).then_inc(inp_l, 1)

            dve.wait_ge(x_in[0], 16)
            statistics(0, 4)
            dve.wait_ge(x_in[1], 16)
            statistics(4, 6)
            norms(0, 0, 4)
            statistics(6, T - 1)
            dve.wait_ge(x_in[2], 32)
            statistics(T - 1, T)
            dve.wait_ge(gat_in, 32)
            for k in range(KC):
                for s in range(2):
                    link(nc.vector.tensor_tensor_reduce(out=wa_out[:, :], in0=gw_sb[:, k, :], in1=ga_sb[:, s, :], scale=W_SCALE,
                                                        scalar=0.0, op0=ALU.mult, op1=ALU.add, accum_out=wa[:, k, s:s + 1]))
            norms(1, 4, T)
            link(nc.vector.tensor_copy(wa_parts[:, 0, :, :], wa[:, :, :]))
            link(nc.vector.tensor_tensor(wa_parts[:, 1, :, :], wa[:, :, :], wa_parts[:, 0, :, :], ALU.subtract))
            for h in range(2):
                for k in range(KC):
                    ins = nc.vector.tensor_copy(wa_rep[:, h, k, :, :], wa_parts[:, h, k, :].unsqueeze(2).broadcast_to((P, 2, P)))
            ins.then_inc(wa_ready, 1)
            for t in range(T):
                inp_low(t)
                if t == 7:
                    weight_lo(0)
            weight_lo(1)
            weight_lo(2)
            dve.wait_ge(st_cols_ready, 1)
            nc.vector.tensor_scalar(st_col[:, :, :], t_ps[:, NP:NP + 2 * T].rearrange("p (t s) -> p t s", s=2), 1.0 / (X_SCALE * W_SCALE),
                                    None, ALU.mult).then_inc(tcols, 1)
            dve.wait_ge(tcols, 1)
            nc.vector.tensor_scalar(t_ramp[:, :], st_col[:, :, 1], 1.0 - SLOPE, None, ALU.mult).then_inc(tcols, 1)
            nc.vector.tensor_scalar(slope_s[:, :], st_col[:, :, 0], -SLOPE, None, ALU.mult)
            r, q = t_rest[:, 0, :], t_rest[:, 1, :]
            dve.wait_ge(consts, 1)
            link(nc.vector.tensor_scalar(r, st_col[:, :, 1], SLOPE, None, ALU.mult))
            link(nc.vector.tensor_copy(t_parts[:, :, 3], r))
            link(nc.vector.tensor_tensor(q, r, t_parts[:, :, 3], ALU.subtract))
            link(nc.vector.tensor_copy(t_parts[:, :, 4], q))
            nc.vector.tensor_tensor(t_parts[:, :, 5], q, t_parts[:, :, 4], ALU.subtract).then_inc(tcols, 1)

            prep = Chain(dve, prep_chain, PREP_STEPS)

            def column(cols, t):
                return cols[:, t:t + 1] if isinstance(t, int) else cols[:, bass.ds(t, 1)]

            def prepare(t, last=False):
                prep.tile(t)
                dve.wait_ge(adj_in, (T + 1) * 16 if last else (t + 1) * 16)
                after(dve, q_ready[1], NU * t)
                nc.vector.tensor_scalar(madj[:, 0:N], adj_sb[:, :], 0.0, -BIG, ALU.is_le, ALU.mult).then_inc(madj_ready, 1)
                dve.wait_ge(madj_ready, t + 1)
                hold()
                a, lr, q, r = stat[:, 0:2], stat[:, 2:4], stat[:, 4:6], stat[:, 6:8]
                top, neg_bottom = stat[:, 8:9], stat[:, 9:10]
                prep.link(nc.vector.tensor_tensor_reduce(out=ttr_out[:, :], in0=madj[:, 0:N], in1=t_row[:, 0:N], scale=1.0,
                                                         scalar=-2 * BIG, op0=ALU.add, op1=ALU.max, accum_out=top))
                hold()
                prep.link(nc.vector.tensor_tensor_reduce(out=ttr_out[:, :], in0=madj[:, 0:N], in1=t_row[:, 0:N], scale=1.0,
                                                         scalar=-2 * BIG, op0=ALU.subtract, op1=ALU.max, accum_out=neg_bottom))
                s = column(st_col[:, :, 0], t)
                nc.vector.tensor_tensor(stat[:, 0:1], top, s, ALU.add)
                nc.vector.tensor_scalar(mcol[:, 0, ROWS - 1:ROWS], top, NO_NEIGHBOUR, None, ALU.is_lt)
                nc.vector.tensor_scalar(mcol[:, 1, ROWS - 1:ROWS], top, NO_NEIGHBOUR, None, ALU.is_lt)
                prep.link(nc.vector.tensor_tensor(stat[:, 1:2], s, neg_bottom, ALU.subtract))
                prep.link(nc.vector.scalar_tensor_tensor(out=lr, in0=a, scalar=SLOPE, in1=a, op0=ALU.mult, op1=ALU.max))
                prep.link(nc.vector.scalar_tensor_tensor(out=r, in0=lr, scalar=column(slope_s, t), in1=signs[:, :], op0=ALU.add, op1=ALU.mult))
                prep.link(nc.vector.tensor_scalar(r, r, P_LOG_SCALE, None, ALU.add))
                prep.link(nc.vector.tensor_copy(mcol[:, :, 0], r))
                prep.link(nc.vector.tensor_tensor(q, r, mcol[:, :, 0], ALU.subtract))
                prep.link(nc.vector.tensor_copy(mcol[:, :, 1], q))
                nc.vector.tensor_tensor(mcol[:, :, 2], q, mcol[:, :, 1], ALU.subtract).then_inc(mcol_ready, 1)
                prep.done()

            def scores(t, u):
                j0, n = UNITS[u]
                w = n * P
                after(dve, plo_done, (NU * t, NU * (t - 1) + 2, NU * t + 1)[u])
                dve.wait_ge(ramp_ready, T * t + j0 + n)
                for s in range(2):
                    dve.wait_ge(q_ready[s], NU * t + u + 1)
                    q3 = q_ps[s][:, 0:w].rearrange("p (j i) -> p j i", i=P)
                    o3 = prob[:, u % 2, s, 0:w].rearrange("p (j i) -> p j i", i=P)
                    nc.vector.tensor_tensor(o3, q3, ramp[:, j0:j0 + n, :], ALU.subtract if s else ALU.add).then_inc(z_done[s], 1)

            tails = Chain(dve, tail_chain, TAIL_STEPS)

            def tail_start(t):
                tails.tile(t)
                dve.wait_ge(att_done, NU * (t + 1))
                nc.vector.reciprocal(stat[:, 12:13], acc_ps[0][:, C:VW])
                tails.link(nc.vector.reciprocal(stat[:, 13:14], acc_ps[1][:, C:VW]))
                tails.link(nc.vector.tensor_tensor(stat[:, 14:16], stat[:, 12:14], unscale[:, :], ALU.mult))
                tails.link(nc.vector.tensor_scalar(new[:, :], acc_ps[0][:, 0:C], stat[:, 14:15], None, ALU.mult))
                nc.vector.scalar_tensor_tensor(out=new[:, :], in0=acc_ps[1][:, 0:C], scalar=stat[:, 15:16], in1=new[:, :],
                                               op0=ALU.mult, op1=ALU.add).then_inc(acc_used, 1)
                dve.wait_ge(acc_used, t + 1)
                nc.vector.tensor_scalar(elu[:, :], new[:, :], 0.0, None, ALU.min).then_inc(new_neg, 1)
                xt = xall[:, t, :] if isinstance(t, int) else xall[:, bass.ds(t, 1), :].rearrange("p a c -> p (a c)")
                tails.link(nc.vector.scalar_tensor_tensor(out=x1[:, :], in0=new[:, :], scalar=0.0, in1=xt, op0=ALU.max, op1=ALU.add))

            def tail_middle(t):
                dve.wait_ge(elu_exp, t + 1)
                tails.link(nc.vector.scalar_tensor_tensor(out=x1[:, :], in0=elu[:, :], scalar=-1.0, in1=x1[:, :], op0=ALU.add, op1=ALU.add))
                tails.link(nc.vector.bn_stats(bn[:, :], x1[:, :]))
                hold()
                tails.link(nc.vector.bn_aggr(mv[:, 0:2], bn[:, :]))
                nc.vector.tensor_scalar(mv[:, 2:3], mv[:, 1:2], 1.0 + EPS, EPS * EPS, ALU.mult, ALU.add).then_inc(stats1, 1)

            def tail_end(t):
                dve.wait_ge(rstd1, t + 1)
                after(dve, flat_tr, t)
                nc.vector.tensor_scalar(y[:, :], x1[:, :], mv[:, 0:1], mv[:, 3:4], ALU.subtract, ALU.mult).then_inc(y_ready, 1)
                tails.done()

            gates_c = Chain(dve, gate_chain, GATE_STEPS)

            def gate(t):
                gates_c.tile(t)
                dve.wait_ge(logits, t + 1)
                nc.vector.scalar_tensor_tensor(out=gl[:, :], in0=logit_ps, scalar=1.0 / X_SCALE, in1=gate_bias[:, :],
                                               op0=ALU.mult, op1=ALU.add).then_inc(gl_done, 1)
                dve.wait_ge(gl_done, t + 1)
                nc.vector.tensor_scalar(pen[:, 0:1], gl[:, 1:2], gl[:, 0:1], -BIG, ALU.is_gt, ALU.mult)
                gates_c.link(nc.vector.tensor_scalar(pen[:, 1:2], gl[:, 1:2], gl[:, 0:1], -BIG, ALU.is_le, ALU.mult))
                for g in range(G):
                    e = slice(g * EG, (g + 1) * EG)
                    ins = nc.vector.tensor_scalar(z8[:, e], gl[:, G + g * EG:G + (g + 1) * EG], pen[:, g:g + 1], None, ALU.add)
                gates_c.link(ins)
                nc.vector.tensor_reduce(route[:, 0:1], z8[:, :], AX_X, ALU.max, negate=True).then_inc(negmax, 1)
                z_j = z8[:, :].unsqueeze(1).broadcast_to((P, E, E))
                z_i = z8[:, :].unsqueeze(2).broadcast_to((P, E, E))
                nc.vector.tensor_tensor(cmp_gt[:, :, :], z_j, z_i, ALU.is_gt)
                gates_c.link(nc.vector.tensor_tensor(cmp_eq[:, :, :], z_j, z_i, ALU.is_equal))
                gates_c.link(nc.vector.tensor_tensor(cmp_eq[:, :, :], cmp_eq[:, :, :], earlier[:, :, :], ALU.mult))
                gates_c.link(nc.vector.tensor_tensor(cmp_gt[:, :, :], cmp_gt[:, :, :], cmp_eq[:, :, :], ALU.add))
                gates_c.link(nc.vector.tensor_reduce(picked[:, :], cmp_gt[:, :, :], AX_X, ALU.add))
                gates_c.link(nc.vector.tensor_scalar(picked[:, :], picked[:, :], 2.0, None, ALU.is_lt))
                after(dve, cnt_tr, t)
                nc.vector.tensor_scalar(cnt[:, 0:E], picked[:, :], CNT_SCALE, None, ALU.mult).then_inc(cnt_ready, 1)
                dve.wait_ge(e8_done, t + 1)
                gates_c.link(nc.vector.tensor_tensor_reduce(out=comb[:, :], in0=picked[:, :], in1=e8[:, :], scale=1.0, scalar=0.0,
                                                            op0=ALU.mult, op1=ALU.add, accum_out=route[:, 2:3]))
                gates_c.link(nc.vector.scalar_tensor_tensor(out=route[:, 3:4], in0=route[:, 1:2], scalar=TOP_EPS, in1=route[:, 2:3],
                                                            op0=ALU.mult, op1=ALU.add))
                gates_c.link(nc.vector.reciprocal(route[:, 4:5], route[:, 3:4]))
                nc.vector.tensor_scalar(comb[:, :], comb[:, :], route[:, 4:5], 1.0 / (H_SCALE * W_SCALE), ALU.mult, ALU.mult).then_inc(comb_ready, 1)
                gates_c.done()

            swi = Chain(dve, swiglu_chain, SWIGLU_STEPS)

            def swiglu(t, w):
                if w == 0:
                    swi.tile(t)
                a, b = f_ps[2 - 2 * w], f_ps[3 - 2 * w]
                dve.wait_ge(tanh_done[w], t + 1)
                swi.link(nc.vector.scalar_tensor_tensor(out=gact[:, :], in0=gact[:, :], scalar=1.0, in1=a, op0=ALU.add, op1=ALU.mult))
                after(dve, hlo_done[1 - w], t + w)
                nc.vector.scalar_tensor_tensor(out=hid[:, :], in0=b, scalar=0.5 * H_SCALE / (X_SCALE * W_SCALE) ** 2, in1=gact[:, :],
                                               op0=ALU.mult, op1=ALU.mult).then_inc(hid_done[w], 1)

            def add_shared(t):
                dve.wait_ge(so_mm, t + 1)
                after(dve, out_stored, 16 * t)
                nc.vector.scalar_tensor_tensor(out=acc_o[:, :], in0=f_ps[3][:, 0:C], scalar=1.0 / (H_SCALE * W_SCALE), in1=x1[:, :],
                                               op0=ALU.mult, op1=ALU.add).then_inc(so_used, 1)

            def add_pair(t, p):
                bank = f_ps[PAIR_BANK[p]]
                if p == 0:
                    dve.wait_ge(comb_ready, t + 1)
                    dve.wait_ge(so_used, t + 1)
                else:
                    dve.wait_ge(pair_used, NPAIR * t + p)
                dve.wait_ge(pair_mm, NPAIR * t + p + 1)
                nc.vector.scalar_tensor_tensor(out=acc_o[:, :], in0=bank[:, 0:C], scalar=comb[:, 2 * p:2 * p + 1],
                                               in1=acc_o[:, :], op0=ALU.mult, op1=ALU.add).then_inc(half_added, 1)
                dve.wait_ge(half_added, NPAIR * t + p + 1)
                nc.vector.scalar_tensor_tensor(out=acc_o[:, :], in0=bank[:, C:2 * C], scalar=comb[:, 2 * p + 1:2 * p + 2],
                                               in1=acc_o[:, :], op0=ALU.mult, op1=ALU.add).then_inc(pair_used, 1)

            def tile(t, attn, ffn, more, last_next=False):
                f = t - 1
                if attn:
                    scores(t, 0)
                    scores(t, 1)
                if not (isinstance(t, int) and t < 2):
                    add_pair(f - 1, 3)
                if not ffn:
                    dve.wait_ge(mean_mm, 1)
                    nc.vector.tensor_scalar(mean_f[:, :, :], mean_ps[:, :].rearrange("p (s c) -> p s c", s=2), 1.0 / N, None,
                                            ALU.mult).then_inc(mean_done, 1)
                if ffn:
                    gate(f)
                    swiglu(f, 0)
                if attn:
                    scores(t, 2)
                    if not ffn:
                        dve.wait_ge(mean_done, 2)
                        nc.vector.tensor_tensor(mean_lo[:, :, :], mean_f[:, :, :], mean_hi[:, :, 0:C], ALU.subtract).then_inc(mean_done, 1)
                if ffn:
                    swiglu(f, 1)
                    swi.done()
                if more:
                    prepare(t + 1, last_next)
                if ffn:
                    add_shared(f)
                if attn:
                    tail_start(t)
                if ffn:
                    add_pair(f, 0)
                if attn:
                    tail_middle(t)
                if ffn:
                    add_pair(f, 1)
                if attn:
                    tail_end(t)
                if ffn:
                    add_pair(f, 2)

            def v_low(j):
                dve.wait_ge(vh_done, j + 1)
                nc.vector.scalar_tensor_tensor(out=v_lo[:, j, :, :], in0=v_ps[j % 2].rearrange("p (s c) -> p s c", s=2),
                                               scalar=V_SCALE / (X_SCALE * W_SCALE), in1=v_hi[:, j, :, 0:C],
                                               op0=ALU.mult, op1=ALU.subtract).then_inc(vl_done, 1)

            by_dve = [n for n in range(3, len(weights)) if n not in BY_POOL]
            v_low(0)
            v_low(1)
            dve.wait_ge(rows_done, 1)
            prepare(0)
            for j in range(2, T):
                v_low(j)
                if by_dve and by_dve[0] <= j + 2:
                    weight_lo(by_dve.pop(0))
            while by_dve:
                weight_lo(by_dve.pop(0))
            dve.wait_ge(bias_done, 1)
            nc.vector.tensor_scalar(lnsb[:, :, :], lnsb[:, :, :], X_SCALE, None, ALU.mult).then_inc(ln_scaled, 1)
            nc.vector.scalar_tensor_tensor(out=bias_lo[:, :], in0=bias_rows[:, :], scalar=H_SCALE * W_SCALE / CNT_SCALE, in1=bias_hi[:, :],
                                           op0=ALU.mult, op1=ALU.subtract).then_inc(bias_done, 1)
            tile(0, True, False, True)
            tile(1, True, True, True)
            with dve.Fori(2, T - 2) as t:
                tile(t, True, True, True)
            tile(T - 2, True, True, True, last_next=True)
            tile(T - 1, True, True, False)
            tile(T, False, True, False)
            add_pair(T - 1, 3)

        @block.tensor
        def _(pe):
            mm = nc.tensor.matmul
            pe.wait_ge(consts, 1)
            for t in range(T):
                pe.wait_ge(inp_ready, t + 1)
                if t >= 2:
                    pe.wait_ge(inp_l, t - 1)
                for k in range(KC):
                    ins = nc.tensor.transpose(tr_ps[t % 2][:, k * P:(k + 1) * P], inp[:, t, k * P:(k + 1) * P], ident_f[:, :])
                ins.then_inc(inp_tr, 1)
            pe.wait_ge(wa_ready, 1)
            pe.wait_ge(inp_l, T)
            parts = [(k, h, x) for k in range(KC) for h, x in ((0, inp_hi), (0, inp_lo), (1, inp_hi))]
            for t in range(T):
                for n, (k, h, x) in enumerate(parts):
                    ins = mm(t_ps[:, NP + 2 * t:NP + 2 * t + 2], lhsT=x[:, k, t * P:(t + 1) * P], rhs=wa_parts[:, h, k, :],
                             start=(n == 0), stop=(n == len(parts) - 1))
            ins.then_inc(st_cols_ready, 1)
            for row_ps, s in ((t_ps, 1), (s_ps, 0)):
                for n0 in range(0, NP, 512):
                    n1 = min(n0 + 512, NP)
                    if s == 1 and n1 == NP:
                        pe.wait_ge(tcols, 1)
                    for n, (k, h, x) in enumerate(parts):
                        ins = mm(row_ps[:, n0:n1], lhsT=wa_rep[:, h, k, s, :], rhs=x[:, k, n0:n1], start=(n == 0), stop=(n == len(parts) - 1))
            ins.then_inc(st_ready, 1)
            low_done(pe, 0)
            for j in range(T):
                if j >= 2:
                    pe.wait_ge(vl_done, j - 1)
                terms = [(a, b, k) for k in range(KC) for a, b in ((inp_hi, wt_hi), (inp_hi, wt_lo), (inp_lo, wt_hi))]
                for n, (a, b, k) in enumerate(terms):
                    ins = mm(v_ps[j % 2], lhsT=a[:, k, j * P:(j + 1) * P], rhs=b[:, k:k + KC + 1:KC, :],
                             start=(n == 0), stop=(n == len(terms) - 1))
                ins.then_inc(v_mm, 1)

            pe.wait_ge(tcols, 3)
            pe.wait_ge(rows_done, 1)
            for j in range(T):
                ins = nc.tensor.transpose(t_rows_ps[0:6, j * P:(j + 1) * P], t_parts[:, j, :], ident_b[:, :])
            ins.then_inc(t_rows_tr, 1)

            def mrow_part(t):
                pe.wait_ge(mcol_ready, t + 1)
                for s in range(2):
                    ins = nc.tensor.transpose(mrow_ps[0:ROWS, s * P:(s + 1) * P], mcol[:, s, :], ident_b[:, :])
                ins.then_inc(mrow_tr, 1)

            def shifts(t, u):
                j0, n = UNITS[u]
                pe.wait_ge(mrow_ready, t + 1)
                for s in range(2):
                    after(pe, z_done[s], NU * t + u)
                    for j in range(n):
                        o = q_ps[s][:, j * P:(j + 1) * P]
                        mm(o, lhsT=t_rows[:, j0 + j, :], rhs=mrow[0:6, s, :], start=True, stop=False)
                        ins = mm(o, lhsT=madj[:, (j0 + j) * P:(j0 + j + 1) * P], rhs=ident_b[:, :], start=False, stop=True)
                    ins.then_inc(q_ready[s], 1)

            def attend(t, u):
                j0, n = UNITS[u]
                pe.wait_ge(plo_done, NU * t + u + 1)
                if u == 0:
                    after(pe, acc_used, t)
                for s in range(2):
                    for j in range(n):
                        i = slice(j * P, (j + 1) * P)
                        mm(acc_ps[s][:, 0:VW], lhsT=p_hi[:, u, s, i], rhs=v_hi[:, j0 + j, s, 0:VW], start=(j0 + j == 0), stop=False)
                        mm(acc_ps[s][:, 0:C], lhsT=p_hi[:, u, s, i], rhs=v_lo[:, j0 + j, s, :], start=False, stop=False)
                        ins = mm(acc_ps[s][:, 0:VW], lhsT=p_lo[:, u, s, i], rhs=v_hi[:, j0 + j, s, 0:VW], start=False, stop=False)
                    if u == NU - 1:
                        mm(acc_ps[s][:, 0:C], lhsT=mrow[:, s, :], rhs=mean_lo[:, s, :], start=False, stop=False)
                        ins = mm(acc_ps[s][:, 0:VW], lhsT=mrow[:, s, :], rhs=mean_hi[:, s, 0:VW], start=False, stop=True)
                ins.then_inc(att_done, 1)

            def mean_of_v():
                for j in range(T):
                    mm(mean_ps[:, :], lhsT=mean_w[:, :], rhs=v_hi[:, j, :, 0:C], start=(j == 0), stop=False)
                    ins = mm(mean_ps[:, :], lhsT=mean_w[:, :], rhs=v_lo[:, j, :, :], start=False, stop=(j == T - 1))
                ins.then_inc(mean_mm, 1)

            def flat_transposes(t):
                pe.wait_ge(y_ready, t + 1)
                after(pe, pair_used, NPAIR * (t - 1) + 1)
                for k in range(KC):
                    ins = nc.tensor.transpose(f_ps[0][:, k * P:(k + 1) * P], y[:, k * P:(k + 1) * P], ident_f[:, :])
                ins.then_inc(flat_tr, 1)

            def gate_logits(t):
                pe.wait_ge(flat_f, KC * (t + 1))
                for k in range(KC):
                    ins = mm(logit_ps, lhsT=flat[:, k, :], rhs=gates[:, k, :], start=(k == 0), stop=(k == KC - 1))
                ins.then_inc(logits, 1)

            def hidden(t, w):
                pe.wait_ge(flat_l, t + 1)
                for half in range(2):
                    if w == 0:
                        after(pe, pair_used, NPAIR * (t - 1) + 2 + half)
                    elif half == 0:
                        pe.wait_ge(gl_done, t + 1)
                    else:
                        after(pe, pair_used, NPAIR * t)
                    bank = f_ps[2 - 2 * w + half]
                    for c in range(KH):
                        cols = slice(half * H + c * P, half * H + (c + 1) * P)
                        terms = [(a, b, k) for k in range(KC) for a, b in ((in_hi, flat_hi), (in_hi, flat_lo), (in_lo, flat_hi))]
                        for n, (a, b, k) in enumerate(terms):
                            ins = mm(bank[:, c * P:(c + 1) * P], lhsT=a[:, w, k, cols], rhs=b[:, k, :], start=(n == 0), stop=(n == len(terms) - 1))
                ins.then_inc(in_mm[w], 1)

            def counts(t):
                pe.wait_ge(cnt_ready, t + 1)
                pe.wait_ge(hid_done[0], t + 1)
                nc.tensor.transpose(cnt_ps[0:E + 1, 0:P], cnt[:, 0:E + 1], ident_h[:, :]).then_inc(cnt_tr, 1)

            def shared_out(t):
                pe.wait_ge(hlo_done[0], t + 1)
                pe.wait_ge(cnt_copied, t + 1)
                o = f_ps[3][:, 0:C]
                for k in range(KH):
                    mm(o, lhsT=h_hi[:, 0, k, :], rhs=so_hi[:, k, :], start=(k == 0), stop=False)
                    mm(o, lhsT=h_hi[:, 0, k, :], rhs=so_lo[:, k, :], start=False, stop=False)
                    mm(o, lhsT=h_lo[:, 0, k, :], rhs=so_hi[:, k, :], start=False, stop=False)
                mm(o, lhsT=cnt_t[:, :], rhs=bias_lo[:, :], start=False, stop=False)
                mm(o, lhsT=cnt_t[:, :], rhs=bias_hi[:, :], start=False, stop=True).then_inc(so_mm, 1)

            def expert_pair(t, p):
                pe.wait_ge(hlo_done[1], t + 1)
                if p == 1:
                    pe.wait_ge(cnt_copied, t + 1)
                if p == 2:
                    pe.wait_ge(so_used, t + 1)
                bank = f_ps[PAIR_BANK[p]]
                cols = slice(2 * p * C, (2 * p + 2) * C)
                for k in range(KH):
                    mm(bank, lhsT=h_hi[:, 1, k, :], rhs=ew[:, 0, k, cols], start=(k == 0), stop=False)
                    mm(bank, lhsT=h_hi[:, 1, k, :], rhs=ew[:, 1, k, cols], start=False, stop=False)
                    ins = mm(bank, lhsT=h_lo[:, 1, k, :], rhs=ew[:, 0, k, cols], start=False, stop=(k == KH - 1))
                ins.then_inc(pair_mm, 1)

            def tile(t, attn, ffn, more):
                f = t - 1
                if attn:
                    shifts(t, 0)
                if ffn:
                    flat_transposes(f)
                if attn:
                    shifts(t, 1)
                if not (isinstance(t, int) and t < 2):
                    if attn:
                        pe.wait_ge(mrow_ready, t + 1)
                    expert_pair(f - 1, 3)
                if not ffn:
                    mean_of_v()
                if ffn:
                    gate_logits(f)
                    hidden(f, 0)
                if attn:
                    attend(t, 0)
                    shifts(t, 2)
                if ffn:
                    hidden(f, 1)
                    counts(f)
                if attn:
                    attend(t, 1)
                if ffn:
                    shared_out(f)
                if attn:
                    if not ffn:
                        pe.wait_ge(mean_done, 3)
                    attend(t, 2)
                if ffn:
                    expert_pair(f, 0)
                if more:
                    mrow_part(t + 1)
                if ffn:
                    expert_pair(f, 1)
                    expert_pair(f, 2)

            mrow_part(0)
            pe.wait_ge(vl_done, T)
            pe.wait_ge(rows_done, 2)
            pe.wait_ge(t_rows_done, 1)
            tile(0, True, False, True)
            low_done(pe, max(n for n in range(len(weights)) if n not in BY_POOL))
            low_done(pe, BY_POOL[-1])
            pe.wait_ge(bias_done, 2)
            tile(1, True, True, True)
            with pe.Fori(2, T - 1) as t:
                tile(t, True, True, True)
            tile(T - 1, True, True, False)
            tile(T, False, True, False)
            expert_pair(T - 1, 3)


def kernel(**inputs):
    import numpy as np
    import concourse.bacc as bacc
    from concourse.bass_utils import run_bass_kernel_spmd

    def arr(name):
        return np.asarray(inputs[name])

    laid = {
        "x": arr("x"),
        "adj": arr("adj"),
        "gat_w": arr("L0_gnn_W"),
        "gat_a": arr("L0_gnn_a").reshape(2, -1),
        "wtrans": arr("L0_gnn_wtrans"),
        "ln_pair": np.stack([arr("L0_ffn_ln_scale"), arr("L0_ffn_ln_bias")]).reshape(2, -1, P).transpose(2, 0, 1),
        "sh_in": arr("L0_ffn_shared_in_w").T,
        "sh_out": arr("L0_ffn_shared_out_w").T,
        "sh_out_b": arr("L0_ffn_shared_out_b"),
        "ex_in": arr("L0_ffn_expert_in_w").T,
        "ex_out": arr("L0_ffn_expert_out_weight").transpose(2, 0, 1),
        "ex_out_b": arr("L0_ffn_expert_out_bias"),
        "group_gate": arr("L0_ffn_group_gate_w").T,
        "expert_gate": arr("L0_ffn_expert_gate_w").T,
        "group_bias": arr("L0_ffn_group_bias"),
        "expert_bias": arr("L0_ffn_expert_bias"),
    }
    nc = bacc.Bacc("TRN2", target_bir_lowering=False, num_devices=1)
    arrays, args = {}, []
    for name, a in laid.items():
        arrays[name] = np.ascontiguousarray(a)
        args.append(nc.dram_tensor(name, a.shape, mybir.dt.from_np(a.dtype), kind="ExternalInput").ap())
    out = nc.dram_tensor("out", laid["x"].shape, F32, kind="ExternalOutput").ap()
    gnn_moe_kernel(nc, *args, out)
    r = run_bass_kernel_spmd(nc, [arrays], core_ids=[0])
    return r.results[0]["out"]
```

```python
from contextlib import ExitStack

import concourse.bass as bass
from concourse import mybir

P = 128
F32 = mybir.dt.float32
F16 = mybir.dt.float16
BF16 = mybir.dt.bfloat16
ALU = mybir.AluOpType
ACT = mybir.ActivationFunctionType
AX_X = mybir.AxisListType.X

BIG = 1e30
FAR = 2.0 ** 96
SLOPE = 0.2
EPS = 1e-5
TOP_EPS = 1e-8
X_SCALE = 2.0 ** 5
W_SCALE = 2.0 ** 8
V_SCALE = 2.0 ** 6
P_LOG_SCALE = 9.010913347279288
H_SCALE = 2.0 ** 4
CNT_SCALE = 2.0 ** 6

PREP_STEPS = 9
TAIL_STEPS = 7
GATE_STEPS = 10


def gnn_moe_kernel(nc, x, adj, gat_w, gat_a, wtrans, ln_pair, sh_in, sh_out, sh_out_b,
                   ex_in, ex_out, ex_out_b, group_gate, expert_gate, group_bias, expert_bias, out):
    N, C = x.shape
    T = -(-N // P)
    NP = T * P
    LAST = N - (T - 1) * P
    KC = C // P
    H = sh_out.shape[0]
    KH = H // P
    E = ex_out.shape[1]
    G = group_gate.shape[1]
    EG = E // G
    VW = C + 1
    UNITS = [(0, 4), (4, 4), (8, T - 8)]
    NU = len(UNITS)
    LOW = 32
    STAGES = 6
    PAIR_BANK = [0, 2, 3, 1]
    END_ORDER = [0, 1, 3, 2], [0, 3, 2, 1]
    NPAIR = E // 2
    TAIL = [((T - 1) * P, 0, 64), ((T - 1) * P + 64, 64, LAST - 64)]
    X_PARTS = [(0, 2), (2, 6), (6, T - 1)]
    NORM_PARTS = [(0, 2), (2, 6), (6, 8), (8, T)]
    assert C == 256 and KH == 4 and E == 8 and T == 11 and LAST > 64

    with ExitStack() as ctx:
        def sb(name, shape, dt=F32):
            return ctx.enter_context(nc.sbuf_tensor(name, shape, dt))

        def sem(name):
            return ctx.enter_context(nc.semaphore(name))

        xall = sb("xall", [P, T, C])
        ramp = sb("ramp", [P, T, P])
        s_row = sb("s_row", [P, NP])
        v_hi = sb("v_hi", [P, T, 2, VW + 1], F16)
        v_lo = sb("v_lo", [P, T, 2, C], F16)
        t_row = sb("t_row", [P, NP])
        st_col = sb("st_col", [P, T, 2])
        in_hi = sb("in_hi", [P, 2, KC, 2 * H], F16)
        in_lo = sb("in_lo", [P, 2, KC, 2 * H], F16)
        so_hi = sb("so_hi", [P, KH, C], F16)
        so_lo = sb("so_lo", [P, KH, C], F16)
        ew = sb("ew", [P, 2, KH, E * C], F16)
        gates = sb("gates", [P, KC, G + E])
        gate_bias = sb("gate_bias", [P, G + E])
        lnsb = sb("lnsb", [P, 2, KC])
        bias_rows = sb("bias_rows", [P, C])
        bias_parts = sb("bias_parts", [P, C], F16)
        ident_b = sb("ident_b", [P, P], BF16)
        ident_h = sb("ident_h", [P, P], F16)
        ident_f = sb("ident_f", [P, P])
        t_parts = sb("t_parts", [P, T, 6], BF16)
        t_rows = sb("t_rows", [P, T, P], BF16)
        t_ramp = sb("t_ramp", [P, T])
        t_pad = sb("t_pad", [P, T])
        slope_s = sb("slope_s", [P, T])
        neg_half = sb("neg_half", [P, T])
        signs = sb("signs", [P, 2])
        unscale = sb("unscale", [P, 2])
        earlier = sb("earlier", [P, E, E])
        adj_sb = sb("adj_sb", [P, N])
        madj = sb("madj", [P, NP], BF16)
        ttr_out = sb("ttr_out", [P, N], BF16)
        stat = sb("stat", [P, 16])
        mcol = sb("mcol", [P, 2, P], BF16)
        mrow = sb("mrow", [P, 2, P], BF16)
        prob_size, part_size = 2 * 2 * 4 * P, NU * 2 * 4 * P
        work = sb("work", [P, prob_size + part_size])
        prob = work[:, 0:prob_size].rearrange("p (b s n) -> p b s n", b=2, s=2)
        p_parts = work[:, prob_size:prob_size + part_size].bitcast(F16)
        p_hi, p_lo = (p_parts[:, h * part_size:(h + 1) * part_size].rearrange("p (u s n) -> p u s n", u=NU, s=2)
                      for h in range(2))
        tail_sb = sb("tail_sb", [P, 4, C])
        new, elu, x1, y = (tail_sb[:, n, :] for n in range(4))
        bn = sb("bn", [P, 6])
        mv = sb("mv", [P, 4])
        carrier = sb("carrier", [1, 1])
        flat = sb("flat", [P, KC, P])
        flat_hi = sb("flat_hi", [P, KC, P], F16)
        flat_lo = sb("flat_lo", [P, KC, P], F16)
        gl = sb("gl", [P, G + E])
        pen = sb("pen", [P, G])
        z8 = sb("z8", [P, E])
        cmp_gt = sb("cmp_gt", [P, E, E])
        cmp_eq = sb("cmp_eq", [P, E, E])
        route = sb("route", [P, 8])
        e8 = sb("e8", [P, E])
        picked = sb("picked", [P, E])
        comb = sb("comb", [P, E])
        cnt = sb("cnt", [P, P], F16)
        cnt_t = sb("cnt_t", [P, P], F16)
        gact = sb("gact", [P, KH * P])
        hid = sb("hid", [P, KH * P])
        h_hi = sb("h_hi", [P, 2, KH, P], F16)
        h_lo = sb("h_lo", [P, 2, KH, P], F16)
        acc_o = sb("acc_o", [P, C])
        stage = sb("stage", [P, STAGES, 1024])
        words = [0]

        def early(n):
            words[0] += n
            return work[:, words[0] - n:words[0]]

        inp = early(T * C).rearrange("p (t c) -> p t c", c=C)
        inp_hi = sb("inp_hi", [P, KC, NP], F16)
        inp_lo = sb("inp_lo", [P, KC, NP], F16)
        wt_hi = sb("wt_hi", [P, 2 * KC, C], F16)
        wt_lo = sb("wt_lo", [P, 2 * KC, C], F16)
        gw_sb = early(KC * C).rearrange("p (k c) -> p k c", c=C)
        ga_sb = early(2 * C).rearrange("p (k c) -> p k c", c=C)
        wa_out = early(C)
        row_sum = sb("row_sum", [P, 2, KC])
        row_mean = sb("row_mean", [P, KC])
        summed = early(NP // 2).bitcast(F16)
        wa = sb("wa", [P, KC, 2])
        wa_parts = sb("wa_parts", [P, 2, KC, 2], F16)
        wa_rep = sb("wa_rep", [P, 2, KC, 2, P], F16)
        bn0 = sb("bn0", [P, T, 6])
        mv0 = sb("mv0", [P, T, 2])
        rs0 = sb("rs0", [P, T])
        norm0 = sb("norm0", [P, 2, T])
        t_rest = sb("t_rest", [P, 2, T])

        psum = ctx.enter_context(nc.psum_tensor("psum", [P, 8, 512], F32))
        q_ps = [psum[:, 0, :], psum[:, 1, :]]
        acc_ps = [psum[:, 2, :], psum[:, 3, :]]
        f_ps = [psum[:, 4 + i, :] for i in range(4)]
        s_ps = psum[:, 2, :]
        s_rest_ps = psum[:, 6:8, :].rearrange("p b n -> p (b n)")
        t_ps = psum[:, 5:8, :].rearrange("p b n -> p (b n)")
        tr_ps = [psum[:, n, 0:KC * P] for n in (0, 3, 4, 7)]
        st_cols_ps = psum[:, 1, 0:2 * T]
        V_BANK = [0, 4, 6, 7, 0, 4, 6, 7, 3, 4, 6]
        v_ps = [psum[:, n, :] for n in V_BANK]
        mrow_ps = f_ps[1].bitcast(BF16)
        t_rows_ps = psum[:, 2:4, :].rearrange("p b n -> p (b n)").bitcast(BF16)
        logit_ps = f_ps[0][:, C:C + G + E]
        last_logit_ps = acc_ps[0][:, 0:G + E]
        cnt_ps = f_ps[2].bitcast(F16)

        x_in = [sem(f"x_in{i}") for i in range(len(X_PARTS) + 1)]
        gat_in = sem("gat_in")
        small_in = sem("small_in")
        staged = [sem(f"staged{n}") for n in range(STAGES)]
        x_pad = sem("x_pad")
        zeros = sem("zeros")
        consts = sem("consts")
        pool_chain = sem("pool_chain")
        stats0 = sem("stats0")
        rstd0 = sem("rstd0")
        start_chain = sem("start_chain")
        wa_ready = sem("wa_ready")
        inp_ready = sem("inp_ready")
        inp_tr = sem("inp_tr")
        inp_h = sem("inp_h")
        normed0 = sem("normed0")
        rows_done = sem("rows_done")
        inp_l = sem("inp_l")
        t_mm = sem("t_mm")
        s_mm = sem("s_mm")
        sums_ready = sem("sums_ready")
        row_mean_done = sem("row_mean_done")
        st_cols_ready = sem("st_cols_ready")
        tcols = sem("tcols")
        ramp_ready = sem("ramp_ready")
        v_mm = sem("v_mm")
        vh_done = sem("vh_done")
        vl_done = sem("vl_done")
        t_rows_tr = sem("t_rows_tr")
        t_rows_done = sem("t_rows_done")
        w_hi = sem("w_hi")
        w_lo = sem("w_lo")
        w_lo_pool = sem("w_lo_pool")
        w_pool_chain = sem("w_pool_chain")
        bias_done = sem("bias_done")
        ln_scaled = sem("ln_scaled")
        adj_in = sem("adj_in")
        madj_ready = sem("madj_ready")
        prep_chain = sem("prep_chain")
        mcol_ready = sem("mcol_ready")
        mrow_tr = sem("mrow_tr")
        mrow_ready = sem("mrow_ready")
        q_ready = [sem("q_ready0"), sem("q_ready1")]
        z_done = [sem("z_done0"), sem("z_done1")]
        exp_done = sem("exp_done")
        phi_done = sem("phi_done")
        plo_done = sem("plo_done")
        att_done = sem("att_done")
        tail_chain = sem("tail_chain")
        acc_used = sem("acc_used")
        new_neg = sem("new_neg")
        elu_exp = sem("elu_exp")
        stats1 = sem("stats1")
        rstd1 = sem("rstd1")
        y_ready = sem("y_ready")
        flat_tr = sem("flat_tr")
        flat_f = sem("flat_f")
        flat_h = sem("flat_h")
        flat_l = sem("flat_l")
        logits = sem("logits")
        gl_done = sem("gl_done")
        gate_chain = sem("gate_chain")
        gact_done = sem("gact_done")
        negmax = sem("negmax")
        e8_done = sem("e8_done")
        cnt_ready = sem("cnt_ready")
        cnt_tr = sem("cnt_tr")
        cnt_copied = sem("cnt_copied")
        in_mm = [sem("in_mm_shared"), sem("in_mm_expert")]
        tanh_done = [sem("tanh_shared"), sem("tanh_expert")]
        hid_done = [sem("hid_shared"), sem("hid_expert")]
        hhi_done = [sem("hhi_shared"), sem("hhi_expert")]
        hlo_done = [sem("hlo_shared"), sem("hlo_expert")]
        so_mm = sem("so_mm")
        so_used = sem("so_used")
        comb_ready = sem("comb_ready")
        half_added = sem("half_added")
        pair_mm = sem("pair_mm")
        pair_used = sem("pair_used")
        out_stored = sem("out_stored")

        def after(eng, s, n):
            if not isinstance(n, int) or n > 0:
                eng.wait_ge(s, n)

        def hold():
            nc.vector.memset(carrier[:, :], 0.0)

        class Chain:
            def __init__(self, eng, s, per_tile):
                self.eng, self.s, self.per_tile = eng, s, per_tile

            def tile(self, t):
                self.t, self.k = t, 0

            def link(self, ins):
                self.k += 1
                ins.then_inc(self.s, 1)
                self.eng.wait_ge(self.s, self.t * self.per_tile + self.k)

            def done(self):
                assert self.k == self.per_tile, (self.s, self.k)

        def rows(t):
            return LAST if isinstance(t, int) and t == T - 1 else P

        def t_is_end(t):
            return isinstance(t, int) and t == T - 1

        def by_chunk(ap, r):
            return ap[:, :].rearrange("p (k n) -> p k n", n=P)[:, :, 0:r]

        def scored(ap, t, u):
            return ap[:, :, 0:UNITS[u][1] * P].rearrange("p s (j i) -> p s j i", i=P)[:, :, :, 0:rows(t)]

        def weight_list():
            lst = [(wtrans.rearrange("(b p) c -> p b c", p=P), wt_hi, wt_lo)]
            for w, src in ((0, sh_in), (1, ex_in)):
                for k in range(KC):
                    lst.append((src[k * P:(k + 1) * P, :], in_hi[:, w, k, :], in_lo[:, w, k, :]))
            lst.append((sh_out.rearrange("(k p) c -> p k c", p=P), so_hi[:, :, :], so_lo[:, :, :]))
            for half in range(2):
                for k in range(KH):
                    e = slice(half * E // 2, (half + 1) * E // 2)
                    c = slice(half * E // 2 * C, (half + 1) * E // 2 * C)
                    lst.append((ex_out[k * P:(k + 1) * P, e, :], ew[:, 0, k, c], ew[:, 1, k, c]))
            return lst

        weights = weight_list()
        BY_POOL = [2, 3, 4, 5, 8, 10, 12]
        BY_ACT_DVE = [n for n in range(len(weights)) if n not in BY_POOL]

        def low_done(eng, n):
            if n in BY_POOL:
                eng.wait_ge(w_lo_pool, BY_POOL.index(n) + 1)
            else:
                eng.wait_ge(w_lo, BY_ACT_DVE.index(n) + 1)

        def stage_view(n, like):
            v = stage[:, n % STAGES, :]
            if len(like.shape) == 2:
                return v
            return v.rearrange("p (a b) -> p a b", b=like.shape[2])

        def flat_free(ap):
            return ap if len(ap.shape) == 2 else ap.rearrange("p a b -> p (a b)")

        block = ctx.enter_context(nc.Block())

        @block.sync
        def _(sp):
            for n, (a, b) in enumerate(X_PARTS):
                sp.dma_start(xall[:, a:b, :], x[a * P:b * P, :].rearrange("(t p) c -> p t c", p=P)).then_inc(x_in[n], 16)
            sp.wait_ge(x_pad, 1)
            for row, part, n in TAIL:
                sp.dma_start(xall[part:part + n, T - 1, :], x[row:row + n, :]).then_inc(x_in[-1], 16)

            def load_weight(n):
                src = weights[n][0]
                if n >= STAGES:
                    low_done(sp, n - STAGES)
                sp.dma_start(stage_view(n, src), src).then_inc(staged[n % STAGES], 16)

            sp.dma_start(gw_sb[:, :, :], gat_w.rearrange("(k p) c -> p k c", p=P)).then_inc(gat_in, 16)
            sp.dma_start(ga_sb[:, :, :], gat_a.partition_broadcast(P)).then_inc(gat_in, 16)
            load_weight(0)
            sp.dma_start(adj_sb[:, :], adj[0:P, :]).then_inc(adj_in, 16)
            for n in range(1, STAGES):
                load_weight(n)
            sp.dma_start(gates[:, :, 0:G], group_gate.rearrange("(k p) g -> p k g", p=P)).then_inc(small_in, 16)
            sp.dma_start(gates[:, :, G:G + E], expert_gate.rearrange("(k p) g -> p k g", p=P)).then_inc(small_in, 16)
            sp.dma_start(gate_bias[:, 0:G], group_bias.partition_broadcast(P)).then_inc(small_in, 16)
            sp.dma_start(gate_bias[:, G:G + E], expert_bias.partition_broadcast(P)).then_inc(small_in, 16)
            sp.dma_start(lnsb[:, :, :], ln_pair).then_inc(small_in, 16)
            sp.wait_ge(zeros, 1)
            for r in (0, LOW):
                sp.dma_start(bias_rows[r:r + E, :], ex_out_b).then_inc(small_in, 16)
                sp.dma_start(bias_rows[r + E:r + E + 1, :], sh_out_b.rearrange("(o c) -> o c", o=1)).then_inc(small_in, 16)
            for n in range(STAGES, len(weights)):
                load_weight(n)
                if n == STAGES + 1:
                    sp.wait_ge(madj_ready, 1)
                    sp.dma_start(adj_sb[:, :], adj[P:2 * P, :]).then_inc(adj_in, 16)

            def store(t, row, part, n):
                if isinstance(t, int) and t == T - 1:
                    sp.wait_ge(so_used, T)
                else:
                    sp.wait_ge(pair_used, NPAIR * (t + 1))
                sp.dma_start(out[row:row + n, :] if isinstance(row, int) else out[bass.ds(row, n), :],
                             acc_o[part:part + n, :]).then_inc(out_stored, 16)

            sp.wait_ge(madj_ready, 2)
            sp.dma_start(adj_sb[:, :], adj[2 * P:3 * P, :]).then_inc(adj_in, 16)
            with sp.Fori(2, T - 2) as t:
                sp.wait_ge(madj_ready, t + 1)
                sp.dma_start(adj_sb[:, :], adj[bass.ds((t + 1) * P, P), :]).then_inc(adj_in, 16)
                store(t - 2, (t - 2) * P, 0, P)
            sp.wait_ge(madj_ready, T - 1)
            for row, part, n in TAIL:
                sp.dma_start(adj_sb[part:part + n, :], adj[row:row + n, :]).then_inc(adj_in, 16)
            for t in range(T - 4, T - 1):
                store(t, t * P, 0, P)
            for row, part, n in TAIL:
                store(T - 1, row, part, n)
            sp.wait_ge(out_stored, 16 * (T + 1))

        @block.gpsimd
        def _(pool):
            nc.gpsimd.memset(xall[:, T - 1, :], 0.0).then_inc(x_pad, 1)
            steps = [0]

            def link(ins):
                steps[0] += 1
                ins.then_inc(pool_chain, 1)
                pool.wait_ge(pool_chain, steps[0])

            nc.gpsimd.memset(ident_b[:, :], 0.0)
            nc.gpsimd.memset(ident_h[:, :], 0.0)
            nc.gpsimd.memset(neg_half[:, :], -0.5)
            link(nc.gpsimd.memset(ident_f[:, :], 0.0))
            for m in (ident_f, ident_b, ident_h):
                nc.gpsimd.affine_select(out=m[:, :], in_=m[:, :], compare_op=ALU.not_equal, fill=1.0, base=0,
                                        pattern=[[-1, P]], channel_multiplier=1)
            nc.gpsimd.memset(t_parts[:, :, 0:3], 1.0)
            pool.wait_ge(zeros, 1)
            nc.gpsimd.memset(mcol[:, 0, 3:6], 1.0)
            nc.gpsimd.memset(mcol[:, 1, 3:6], -1.0)
            nc.gpsimd.memset(signs[:, 0:1], -1.0)
            nc.gpsimd.memset(signs[:, 1:2], 1.0)
            nc.gpsimd.memset(unscale[:, 0:1], 1.0 / V_SCALE)
            nc.gpsimd.memset(unscale[:, 1:2], -1.0 / V_SCALE)
            nc.gpsimd.memset(cnt[:, E:E + LOW + 1:LOW], CNT_SCALE)
            nc.gpsimd.memset(v_hi[:, :, :, C:VW + 1], 1.0)
            nc.gpsimd.memset(madj[:, N:N + 1], -FAR)
            nc.gpsimd.memset(madj[:, N + 1:NP], -BIG)
            nc.gpsimd.memset(s_row[:, N:NP], 0.0)
            nc.gpsimd.memset(t_pad[:, :], 0.0)
            nc.gpsimd.memset(t_row[:, N:NP], 0.0)
            link(nc.gpsimd.memset(earlier[:, :, :], 1.0))
            nc.gpsimd.affine_select(out=earlier[:, :, :], in_=earlier[:, :, :], compare_op=ALU.is_gt, fill=0.0,
                                    base=0, pattern=[[1, E], [-1, E]], channel_multiplier=0)
            nc.gpsimd.affine_select(out=t_pad[:, :], in_=t_pad[:, :], compare_op=ALU.is_gt, fill=-BIG,
                                    base=N, pattern=[[-P, T]], channel_multiplier=-1).then_inc(consts, 1)
            for a, b in NORM_PARTS:
                pool.wait_ge(stats0, b)
                link(nc.gpsimd.tensor_scalar(rs0[:, a:b], mv0[:, a:b, 1], EPS, None, ALU.add))
                nc.gpsimd.tensor_tensor(rs0[:, a:b], rs0[:, a:b], neg_half[:, a:b], ALU.pow).then_inc(rstd0, 1)

            def rstd(t):
                pool.wait_ge(stats1, t + 1)
                nc.gpsimd.tensor_tensor(mv[:, 3:4], mv[:, 2:3], neg_half[:, 0:1], ALU.pow).then_inc(rstd1, 1)

            def weight_split(n):
                _, hi, lo = weights[n]
                k = 2 * BY_POOL.index(n)
                pool.wait_ge(staged[n % STAGES], 16 * (n // STAGES + 1))
                st = stage[:, n % STAGES, :]
                nc.gpsimd.tensor_scalar(flat_free(hi), st, W_SCALE, 1.0, ALU.mult, ALU.mult).then_inc(w_pool_chain, 1)
                pool.wait_ge(w_pool_chain, k + 1)
                nc.gpsimd.tensor_scalar(st, st, W_SCALE, 1.0, ALU.mult, ALU.mult).then_inc(w_pool_chain, 1)
                pool.wait_ge(w_pool_chain, k + 2)
                nc.gpsimd.tensor_tensor(flat_free(lo), st, flat_free(hi), ALU.subtract).then_inc(w_lo_pool, 1)

            def lows(t, u):
                pool.wait_ge(phi_done, NU * t + u + 1)
                nc.gpsimd.tensor_tensor(scored(p_lo[:, u], t, u), scored(prob[:, u % 2], t, u), scored(p_hi[:, u], t, u), ALU.subtract).then_inc(plo_done, 1)

            def flat_low(t):
                pool.wait_ge(flat_h, t + 1)
                nc.gpsimd.tensor_tensor(flat_lo[:, :, :], flat[:, :, :], flat_hi[:, :, :], ALU.subtract).then_inc(flat_l, 1)

            def hid_low(t, w):
                pool.wait_ge(hhi_done[w], t + 1)
                r = rows(t)
                nc.gpsimd.tensor_tensor(h_lo[:, w, :, 0:r], by_chunk(hid, r), h_hi[:, w, :, 0:r], ALU.subtract).then_inc(hlo_done[w], 1)

            def tile(t):
                f = t - 1
                flat_low(f)
                lows(t, 0)
                lows(t, 1)
                hid_low(f, 0)
                lows(t, 2)
                hid_low(f, 1)
                if isinstance(t, int) and t == 1:
                    weight_split(BY_POOL[-1])
                rstd(t)

            for n in BY_POOL[:-2]:
                weight_split(n)
            lows(0, 0)
            lows(0, 1)
            lows(0, 2)
            weight_split(BY_POOL[-2])
            rstd(0)
            tile(1)
            with pool.Fori(2, T - 1) as t:
                tile(t)
            tile(T - 1)
            flat_low(T - 1)
            hid_low(T - 1, 1)
            hid_low(T - 1, 0)

        @block.scalar
        def _(act):
            def weight_hi(n):
                src, hi, _ = weights[n]
                act.wait_ge(staged[n % STAGES], 16 * (n // STAGES + 1))
                nc.scalar.activation(flat_free(hi), stage[:, n % STAGES, :], ACT.Copy, scale=W_SCALE).then_inc(w_hi, 1)

            def normalise(t):
                act.wait_ge(normed0, t + 1)
                nc.scalar.activation(inp[:, t, :], xall[:, t, :], ACT.Identity, bias=norm0[:, 1, t:t + 1],
                                     scale=norm0[:, 0, t:t + 1]).then_inc(inp_ready, 1)

            def inp_high(t):
                act.wait_ge(inp_tr, t + 1)
                nc.scalar.activation(inp_hi[:, :, t * P:(t + 1) * P], tr_ps[t % 4].rearrange("p (k n) -> p k n", k=KC),
                                     ACT.Copy).then_inc(inp_h, 1)

            for t in range(T):
                normalise(t)
                if t >= 1:
                    inp_high(t - 1)
                if t == 5:
                    weight_hi(0)
            inp_high(T - 1)

            def row_sums(h, k):
                n = KC * h + k
                after(act, sums_ready, n)
                nc.scalar.activation(summed[:, :], (inp_hi, inp_lo)[h][:, k, :], ACT.Copy, accum_out=row_sum[:, h, k:k + 1]).then_inc(sums_ready, 1)

            weight_hi(1)
            act.wait_ge(inp_h, T)
            row_sums(0, 0)
            row_sums(0, 1)
            act.wait_ge(t_mm, 1)
            nc.scalar.activation(t_row[:, 0:N], t_ps[:, 0:N], ACT.Copy, scale=1.0 / (X_SCALE * W_SCALE)).then_inc(rows_done, 1)

            def v_high(j):
                act.wait_ge(v_mm, j + 1)
                nc.scalar.activation(v_hi[:, j, :, 0:C], v_ps[j].rearrange("p (s c) -> p s c", s=2), ACT.Copy,
                                     scale=V_SCALE / (X_SCALE * W_SCALE)).then_inc(vh_done, 1)

            def ramps(t, j0=0, j1=T):
                i = slice(t * P, (t + 1) * P) if isinstance(t, int) else bass.ds(t * P, P)
                for j in range(j0, j1):
                    nc.scalar.activation(ramp[:, j, :], s_row[:, i], ACT.Relu, bias=t_ramp[:, j:j + 1], scale=1.0 - SLOPE).then_inc(ramp_ready, 1)

            def exps(t, u):
                for s in range(2):
                    act.wait_ge(z_done[s], NU * t + u + 1)
                pr = scored(prob[:, u % 2], t, u)
                nc.scalar.activation(pr, pr, ACT.Exp).then_inc(exp_done, 1)

            def highs(t, u):
                act.wait_ge(exp_done, NU * t + u + 1)
                after(act, att_done, NU * (t - 1) + u + 1)
                nc.scalar.activation(scored(p_hi[:, u], t, u), scored(prob[:, u % 2], t, u), ACT.Copy).then_inc(phi_done, 1)

            def mrow_copy(t):
                act.wait_ge(mrow_tr, t + 1)
                nc.scalar.activation(mrow[:, :, :], mrow_ps[:, 0:2 * P].rearrange("p (s n) -> p s n", s=2), ACT.Copy).then_inc(mrow_ready, 1)

            def elu_part(t):
                act.wait_ge(new_neg, t + 1)
                nc.scalar.activation(elu[:, :], elu[:, :], ACT.Exp).then_inc(elu_exp, 1)

            def flat_part(t):
                act.wait_ge(flat_tr, t + 1)
                ps = f_ps[0][:, 0:KC * P].rearrange("p (k n) -> p k n", k=KC)
                after(act, flat_l, t)
                for k in range(KC):
                    nc.scalar.activation(flat[:, k, :], ps[:, k, :], ACT.Identity, bias=lnsb[:, 1, k:k + 1],
                                         scale=lnsb[:, 0, k:k + 1]).then_inc(flat_f, 1)
                act.wait_ge(flat_f, KC * (t + 1))
                nc.scalar.activation(flat_hi[:, :, :], flat[:, :, :], ACT.Copy).then_inc(flat_h, 1)

            def tanhs(t, w):
                act.wait_ge(in_mm[w], t + 1)
                nc.scalar.activation(by_chunk(gact, rows(t)), by_chunk(f_ps[2 - 2 * w], rows(t)), ACT.Tanh, scale=0.5 / (X_SCALE * W_SCALE)).then_inc(tanh_done[w], 1)

            def hid_high(t, w):
                act.wait_ge(hid_done[w], t + 1)
                after(act, *((so_mm, t) if w == 0 else (pair_mm, NPAIR * t)))
                nc.scalar.activation(h_hi[:, w, :, 0:rows(t)], by_chunk(hid, rows(t)), ACT.Copy).then_inc(hhi_done[w], 1)

            def route_exp(t):
                act.wait_ge(negmax, t + 1)
                nc.scalar.activation(e8[:, :], z8[:, :], ACT.Exp, bias=route[:, 0:1], accum_out=route[:, 1:2]).then_inc(e8_done, 1)

            def cnt_copy(t):
                act.wait_ge(cnt_tr, t + 1)
                nc.scalar.activation(cnt_t[:, :], cnt_ps[:, 0:P], ACT.Copy).then_inc(cnt_copied, 1)

            def first_tile():
                exps(0, 2)
                highs(0, 2)
                weight_hi(6)
                ramps(1)
                mrow_copy(1)
                weight_hi(7)
                elu_part(0)
                act.wait_ge(small_in, 9 * 16)
                nc.scalar.activation(bias_parts[:, :], bias_rows[:, :], ACT.Copy, scale=H_SCALE * W_SCALE / CNT_SCALE).then_inc(bias_done, 1)
                weight_hi(9)
                act.wait_ge(s_mm, 2)
                nc.scalar.activation(s_row[:, 512:N], s_rest_ps[:, 0:N - 512], ACT.Copy, scale=1.0 / (X_SCALE * W_SCALE)).then_inc(rows_done, 1)

            def tile(t, more):
                f = t - 1
                flat_part(f)
                first = isinstance(t, int) and t == 1
                exps(t, 0)
                highs(t, 0)
                if first:
                    weight_hi(11)
                exps(t, 1)
                highs(t, 1)
                if first:
                    weight_hi(13)
                route_exp(f)
                tanhs(f, 0)
                hid_high(f, 0)
                if first:
                    cnt_copy(f)
                exps(t, 2)
                highs(t, 2)
                tanhs(f, 1)
                if not first:
                    cnt_copy(f)
                hid_high(f, 1)
                if first:
                    act.wait_ge(rows_done, 3)
                if more:
                    ramps(t + 1)
                    mrow_copy(t + 1)
                elu_part(t)

            def last_tile():
                f = T - 1
                flat_part(f)
                tanhs(f, 1)
                hid_high(f, 1)
                tanhs(f, 0)
                hid_high(f, 0)
                route_exp(f)
                cnt_copy(f)

            v_high(0)
            act.wait_ge(inp_l, T)
            row_sums(1, 0)
            v_high(1)
            act.wait_ge(s_mm, 1)
            nc.scalar.activation(s_row[:, 0:512], s_ps, ACT.Copy, scale=1.0 / (X_SCALE * W_SCALE)).then_inc(rows_done, 1)
            row_sums(1, 1)
            v_high(2)
            v_high(3)
            act.wait_ge(tcols, 2)
            act.wait_ge(rows_done, 2)
            ramps(0, 0, 4)
            v_high(4)
            act.wait_ge(t_rows_tr, 1)
            nc.scalar.activation(t_rows[0:6, :, :], t_rows_ps[0:6, 0:NP].rearrange("p (t n) -> p t n", n=P), ACT.Copy).then_inc(t_rows_done, 1)
            v_high(5)
            ramps(0, 4, 8)
            mrow_copy(0)
            v_high(6)
            ramps(0, 8, T)
            v_high(7)
            exps(0, 0)
            v_high(8)
            highs(0, 0)
            v_high(9)
            exps(0, 1)
            v_high(10)
            highs(0, 1)
            first_tile()
            act.wait_ge(ln_scaled, 1)
            tile(1, True)
            with act.Fori(2, T - 1) as t:
                tile(t, True)
            tile(T - 1, False)
            last_tile()

        @block.vector
        def _(dve):
            steps = [0]

            def link(ins):
                steps[0] += 1
                ins.then_inc(start_chain, 1)
                dve.wait_ge(start_chain, steps[0])

            def weight_lo(n):
                _, hi, lo = weights[n]
                dve.wait_ge(w_hi, BY_ACT_DVE.index(n) + 1)
                nc.vector.scalar_tensor_tensor(out=flat_free(lo), in0=stage[:, n % STAGES, :], scalar=W_SCALE, in1=flat_free(hi),
                                               op0=ALU.mult, op1=ALU.subtract).then_inc(w_lo, 1)

            for buf in (bias_rows[:, :], mcol[:, :, :], cnt[:, :]):
                nc.vector.memset(buf, 0.0)
            nc.vector.memset(t_rows[:, :, :], 0.0).then_inc(zeros, 1)

            def statistics(a, b):
                for t in range(a, b):
                    link(nc.vector.bn_stats(bn0[:, t, :], xall[:, t, :]))
                    nc.vector.bn_aggr(mv0[:, t, :], bn0[:, t, :]).then_inc(stats0, 1)

            def norms(part):
                a, b = NORM_PARTS[part]
                dve.wait_ge(rstd0, part + 1)
                link(nc.vector.tensor_scalar(norm0[:, 0, a:b], rs0[:, a:b], X_SCALE, None, ALU.mult))
                nc.vector.scalar_tensor_tensor(out=norm0[:, 1, a:b], in0=mv0[:, a:b, 0], scalar=-1.0, in1=norm0[:, 0, a:b],
                                               op0=ALU.mult, op1=ALU.mult).then_inc(normed0, b - a)

            def inp_low(t):
                dve.wait_ge(inp_h, t + 1)
                nc.vector.tensor_tensor(inp_lo[:, :, t * P:(t + 1) * P], tr_ps[t % 4].rearrange("p (k n) -> p k n", k=KC),
                                        inp_hi[:, :, t * P:(t + 1) * P], ALU.subtract).then_inc(inp_l, 1)

            dve.wait_ge(x_in[0], 16)
            statistics(0, 2)
            dve.wait_ge(x_in[1], 16)
            statistics(2, 5)
            norms(0)
            statistics(5, 6)
            dve.wait_ge(gat_in, 32)
            for k in range(KC):
                for s in range(2):
                    link(nc.vector.tensor_tensor_reduce(out=wa_out[:, :], in0=gw_sb[:, k, :], in1=ga_sb[:, s, :], scale=W_SCALE,
                                                        scalar=0.0, op0=ALU.mult, op1=ALU.add, accum_out=wa[:, k, s:s + 1]))
            norms(1)
            link(nc.vector.tensor_copy(wa_parts[:, 0, :, :], wa[:, :, :]))
            link(nc.vector.tensor_tensor(wa_parts[:, 1, :, :], wa[:, :, :], wa_parts[:, 0, :, :], ALU.subtract))
            for h in range(2):
                for k in range(KC):
                    ins = nc.vector.tensor_copy(wa_rep[:, h, k, :, :], wa_parts[:, h, k, :].unsqueeze(2).broadcast_to((P, 2, P)))
            ins.then_inc(wa_ready, 1)
            inp_low(0)
            dve.wait_ge(x_in[2], 16)
            statistics(6, 8)
            for t in range(1, 4):
                inp_low(t)
            statistics(8, T - 1)
            norms(2)
            dve.wait_ge(x_in[3], 32)
            statistics(T - 1, T)
            inp_low(4)
            inp_low(5)
            norms(3)
            for t in range(6, T):
                inp_low(t)
            weight_lo(0)

            def columns():
                dve.wait_ge(st_cols_ready, 1)
                nc.vector.tensor_scalar(st_col[:, :, :], st_cols_ps.rearrange("p (t s) -> p t s", s=2), 1.0 / (X_SCALE * W_SCALE),
                                        None, ALU.mult).then_inc(tcols, 1)
                dve.wait_ge(tcols, 1)
                nc.vector.scalar_tensor_tensor(out=t_ramp[:, :], in0=st_col[:, :, 1], scalar=1.0 - SLOPE, in1=t_pad[:, :],
                                               op0=ALU.mult, op1=ALU.add).then_inc(tcols, 1)
                nc.vector.tensor_scalar(slope_s[:, :], st_col[:, :, 0], -SLOPE, None, ALU.mult)
                r, q = t_rest[:, 0, :], t_rest[:, 1, :]
                link(nc.vector.tensor_scalar(r, st_col[:, :, 1], SLOPE, None, ALU.mult))
                link(nc.vector.tensor_copy(t_parts[:, :, 3], r))
                link(nc.vector.tensor_tensor(q, r, t_parts[:, :, 3], ALU.subtract))
                link(nc.vector.tensor_copy(t_parts[:, :, 4], q))
                nc.vector.tensor_tensor(t_parts[:, :, 5], q, t_parts[:, :, 4], ALU.subtract).then_inc(tcols, 1)

            prep = Chain(dve, prep_chain, PREP_STEPS)

            def column(cols, t):
                return cols[:, t:t + 1] if isinstance(t, int) else cols[:, bass.ds(t, 1)]

            def prepare_mask(t, last=False):
                prep.tile(t)
                dve.wait_ge(adj_in, (T + 1) * 16 if last else (t + 1) * 16)
                after(dve, q_ready[1], NU * t)
                nc.vector.tensor_scalar(madj[:, 0:N], adj_sb[:, :], 0.0, -BIG, ALU.is_le, ALU.mult).then_inc(madj_ready, 1)
                dve.wait_ge(madj_ready, t + 1)

            top, neg_bottom = stat[:, 8:9], stat[:, 9:10]

            def prepare_max(s):
                hold()
                prep.link(nc.vector.tensor_tensor_reduce(out=ttr_out[:, :], in0=madj[:, 0:N], in1=t_row[:, 0:N], scale=1.0,
                                                         scalar=-2 * BIG, op0=(ALU.add, ALU.subtract)[s], op1=ALU.max,
                                                         accum_out=(top, neg_bottom)[s]))

            def prepare_shift(t):
                a, lr, q, r = stat[:, 0:2], stat[:, 2:4], stat[:, 4:6], stat[:, 6:8]
                s = column(st_col[:, :, 0], t)
                nc.vector.tensor_tensor(stat[:, 0:1], top, s, ALU.add)
                prep.link(nc.vector.tensor_tensor(stat[:, 1:2], s, neg_bottom, ALU.subtract))
                prep.link(nc.vector.scalar_tensor_tensor(out=lr, in0=a, scalar=SLOPE, in1=a, op0=ALU.mult, op1=ALU.max))
                prep.link(nc.vector.scalar_tensor_tensor(out=r, in0=lr, scalar=column(slope_s, t), in1=signs[:, :], op0=ALU.add, op1=ALU.mult))
                prep.link(nc.vector.tensor_scalar(r, r, P_LOG_SCALE, FAR, ALU.add, ALU.min))
                prep.link(nc.vector.tensor_copy(mcol[:, :, 0], r))
                prep.link(nc.vector.tensor_tensor(q, r, mcol[:, :, 0], ALU.subtract))
                prep.link(nc.vector.tensor_copy(mcol[:, :, 1], q))
                nc.vector.tensor_tensor(mcol[:, :, 2], q, mcol[:, :, 1], ALU.subtract).then_inc(mcol_ready, 1)
                prep.done()

            def prepare(t, last=False):
                prepare_mask(t, last)
                prepare_max(0)
                prepare_max(1)
                prepare_shift(t)

            def scores(t, u):
                j0, n = UNITS[u]
                w = n * P
                after(dve, plo_done, (NU * t, NU * (t - 1) + 2, NU * t + 1)[u])
                dve.wait_ge(ramp_ready, T * t + j0 + n)
                for s in range(2):
                    dve.wait_ge(q_ready[s], NU * t + u + 1)
                    q3 = q_ps[s][:, 0:w].rearrange("p (j i) -> p j i", i=P)[:, :, 0:rows(t)]
                    o3 = prob[:, u % 2, s, 0:w].rearrange("p (j i) -> p j i", i=P)[:, :, 0:rows(t)]
                    nc.vector.tensor_tensor(o3, q3, ramp[:, j0:j0 + n, 0:rows(t)], ALU.subtract if s else ALU.add).then_inc(z_done[s], 1)

            tails = Chain(dve, tail_chain, TAIL_STEPS)

            def tail_start(t):
                tails.tile(t)
                dve.wait_ge(att_done, NU * (t + 1))
                nc.vector.reciprocal(stat[:, 12:13], acc_ps[0][:, C:VW])
                tails.link(nc.vector.reciprocal(stat[:, 13:14], acc_ps[1][:, C:VW]))
                tails.link(nc.vector.tensor_tensor(stat[:, 14:16], stat[:, 12:14], unscale[:, :], ALU.mult))
                tails.link(nc.vector.tensor_scalar(new[:, :], acc_ps[0][:, 0:C], stat[:, 14:15], None, ALU.mult))
                nc.vector.scalar_tensor_tensor(out=new[:, :], in0=acc_ps[1][:, 0:C], scalar=stat[:, 15:16], in1=new[:, :],
                                               op0=ALU.mult, op1=ALU.add).then_inc(acc_used, 1)
                dve.wait_ge(acc_used, t + 1)
                nc.vector.tensor_scalar(elu[:, :], new[:, :], 0.0, None, ALU.min).then_inc(new_neg, 1)
                xt = xall[:, t, :] if isinstance(t, int) else xall[:, bass.ds(t, 1), :].rearrange("p a c -> p (a c)")
                tails.link(nc.vector.scalar_tensor_tensor(out=x1[:, :], in0=new[:, :], scalar=0.0, in1=xt, op0=ALU.max, op1=ALU.add))

            def tail_middle(t):
                dve.wait_ge(elu_exp, t + 1)
                tails.link(nc.vector.scalar_tensor_tensor(out=x1[:, :], in0=elu[:, :], scalar=-1.0, in1=x1[:, :], op0=ALU.add, op1=ALU.add))
                tails.link(nc.vector.bn_stats(bn[:, :], x1[:, :]))
                hold()
                tails.link(nc.vector.bn_aggr(mv[:, 0:2], bn[:, :]))
                nc.vector.tensor_scalar(mv[:, 2:3], mv[:, 1:2], 1.0 + EPS, EPS * EPS, ALU.mult, ALU.add).then_inc(stats1, 1)

            def tail_end(t):
                dve.wait_ge(rstd1, t + 1)
                after(dve, flat_tr, t)
                nc.vector.tensor_scalar(y[:, :], x1[:, :], mv[:, 0:1], mv[:, 3:4], ALU.subtract, ALU.mult).then_inc(y_ready, 1)
                tails.done()

            gates_c = Chain(dve, gate_chain, GATE_STEPS)

            def gate_start(t, logit_ps):
                gates_c.tile(t)
                dve.wait_ge(logits, t + 1)
                nc.vector.scalar_tensor_tensor(out=gl[:, :], in0=logit_ps, scalar=1.0 / X_SCALE, in1=gate_bias[:, :],
                                               op0=ALU.mult, op1=ALU.add).then_inc(gl_done, 1)

            def gate(t):
                dve.wait_ge(gl_done, t + 1)
                nc.vector.tensor_scalar(pen[:, 0:1], gl[:, 1:2], gl[:, 0:1], -BIG, ALU.is_gt, ALU.mult)
                gates_c.link(nc.vector.tensor_scalar(pen[:, 1:2], gl[:, 1:2], gl[:, 0:1], -BIG, ALU.is_le, ALU.mult))
                for g in range(G):
                    e = slice(g * EG, (g + 1) * EG)
                    ins = nc.vector.tensor_scalar(z8[:, e], gl[:, G + g * EG:G + (g + 1) * EG], pen[:, g:g + 1], None, ALU.add)
                gates_c.link(ins)
                nc.vector.tensor_reduce(route[:, 0:1], z8[:, :], AX_X, ALU.max, negate=True).then_inc(negmax, 1)
                z_j = z8[:, :].unsqueeze(1).broadcast_to((P, E, E))
                z_i = z8[:, :].unsqueeze(2).broadcast_to((P, E, E))
                nc.vector.tensor_tensor(cmp_gt[:, :, :], z_j, z_i, ALU.is_gt)
                gates_c.link(nc.vector.tensor_tensor(cmp_eq[:, :, :], z_j, z_i, ALU.is_equal))
                gates_c.link(nc.vector.tensor_tensor(cmp_eq[:, :, :], cmp_eq[:, :, :], earlier[:, :, :], ALU.mult))
                gates_c.link(nc.vector.tensor_tensor(cmp_gt[:, :, :], cmp_gt[:, :, :], cmp_eq[:, :, :], ALU.add))
                gates_c.link(nc.vector.tensor_reduce(picked[:, :], cmp_gt[:, :, :], AX_X, ALU.add))
                gates_c.link(nc.vector.tensor_scalar(picked[:, :], picked[:, :], 2.0, None, ALU.is_lt))
                after(dve, cnt_tr, t)
                nc.vector.tensor_scalar(cnt[:, 0:2 * LOW].rearrange("p (h n) -> p h n", h=2)[:, :, 0:E],
                                        picked[:, :].unsqueeze(1).broadcast_to((P, 2, E)), CNT_SCALE, None, ALU.mult).then_inc(cnt_ready, 1)
                dve.wait_ge(e8_done, t + 1)
                gates_c.link(nc.vector.tensor_tensor_reduce(out=comb[:, :], in0=picked[:, :], in1=e8[:, :], scale=1.0, scalar=0.0,
                                                            op0=ALU.mult, op1=ALU.add, accum_out=route[:, 2:3]))
                gates_c.link(nc.vector.scalar_tensor_tensor(out=route[:, 3:4], in0=route[:, 1:2], scalar=TOP_EPS, in1=route[:, 2:3],
                                                            op0=ALU.mult, op1=ALU.add))
                gates_c.link(nc.vector.reciprocal(route[:, 4:5], route[:, 3:4]))
                nc.vector.tensor_scalar(comb[:, :], comb[:, :], route[:, 4:5], 1.0 / (H_SCALE * W_SCALE), ALU.mult, ALU.mult).then_inc(comb_ready, 1)
                gates_c.done()

            def swiglu(t, w, first=None):
                first = w == 0 if first is None else first
                r = rows(t)
                a, b, g = by_chunk(f_ps[2 - 2 * w], r), by_chunk(f_ps[3 - 2 * w], r), by_chunk(gact, r)
                dve.wait_ge(tanh_done[w], t + 1)
                nc.vector.scalar_tensor_tensor(out=g, in0=g, scalar=1.0, in1=a, op0=ALU.add, op1=ALU.mult).then_inc(gact_done, 1)
                dve.wait_ge(gact_done, 2 * t + (1 if first else 2))
                after(dve, *((hlo_done[1], t) if first else (hlo_done[1 - w], t + 1)))
                nc.vector.scalar_tensor_tensor(out=by_chunk(hid, r), in0=b, scalar=0.5 * H_SCALE / (X_SCALE * W_SCALE) ** 2, in1=g,
                                               op0=ALU.mult, op1=ALU.mult).then_inc(hid_done[w], 1)

            def add_shared(t):
                dve.wait_ge(so_mm, t + 1)
                after(dve, out_stored, 16 * t)
                nc.vector.scalar_tensor_tensor(out=acc_o[:, :], in0=f_ps[3][:, 0:C], scalar=1.0 / (H_SCALE * W_SCALE), in1=x1[:, :],
                                               op0=ALU.mult, op1=ALU.add).then_inc(so_used, 1)

            def add_pair(t, p, n=None):
                n = p if n is None else n
                bank = f_ps[PAIR_BANK[p]]
                last = isinstance(t, int) and t == T - 1
                so_far = x1 if last and n == 0 else acc_o
                if n == 0:
                    dve.wait_ge(comb_ready, t + 1)
                if n == 0 and last:
                    dve.wait_ge(out_stored, 16 * t)
                elif n == 0:
                    dve.wait_ge(so_used, t + 1)
                else:
                    dve.wait_ge(pair_used, NPAIR * t + n)
                dve.wait_ge(pair_mm, NPAIR * t + n + 1)
                nc.vector.scalar_tensor_tensor(out=acc_o[:, :], in0=bank[:, 0:C], scalar=comb[:, 2 * p:2 * p + 1],
                                               in1=so_far[:, :], op0=ALU.mult, op1=ALU.add).then_inc(half_added, 1)
                dve.wait_ge(half_added, NPAIR * t + n + 1)
                nc.vector.scalar_tensor_tensor(out=acc_o[:, :], in0=bank[:, C:2 * C], scalar=comb[:, 2 * p + 1:2 * p + 2],
                                               in1=acc_o[:, :], op0=ALU.mult, op1=ALU.add).then_inc(pair_used, 1)

            def tile(t, more, last_next=False):
                f = t - 1
                first = isinstance(t, int) and t == 1
                scores(t, 0)
                if first:
                    weight_lo(6)
                    weight_lo(7)
                else:
                    add_pair(f - 1, 3)
                scores(t, 1)
                if first:
                    weight_lo(9)
                gate_start(f, logit_ps)
                gate(f)
                swiglu(f, 0)
                scores(t, 2)
                if first:
                    weight_lo(11)
                    weight_lo(13)
                swiglu(f, 1)
                if more:
                    prepare(t + 1, last_next)
                add_shared(f)
                tail_start(t)
                add_pair(f, 0)
                tail_middle(t)
                add_pair(f, 1)
                tail_end(t)
                add_pair(f, *((END_ORDER[0][2], 2) if t_is_end(t) else (2,)))

            def last_tile():
                f = T - 1
                add_pair(f - 1, END_ORDER[0][3], 3)
                swiglu(f, 1, first=True)
                swiglu(f, 0, first=False)
                gate_start(f, last_logit_ps)
                gate(f)
                for n, p in enumerate(END_ORDER[1]):
                    add_pair(f, p, n)
                dve.wait_ge(so_mm, f + 1)
                dve.wait_ge(pair_used, NPAIR * T)
                nc.vector.scalar_tensor_tensor(out=acc_o[:, :], in0=f_ps[0][:, 0:C], scalar=1.0 / (H_SCALE * W_SCALE), in1=acc_o[:, :],
                                               op0=ALU.mult, op1=ALU.add).then_inc(so_used, 1)

            def v_low(j):
                dve.wait_ge(vh_done, j + 1)
                nc.vector.scalar_tensor_tensor(out=v_lo[:, j, :, :], in0=v_ps[j].rearrange("p (s c) -> p s c", s=2),
                                               scalar=V_SCALE / (X_SCALE * W_SCALE), in1=v_hi[:, j, :, 0:C],
                                               op0=ALU.mult, op1=ALU.subtract).then_inc(vl_done, 1)

            prepare_mask(0)
            weight_lo(1)
            dve.wait_ge(rows_done, 1)
            prepare_max(0)
            v_low(0)
            prepare_max(1)
            v_low(1)
            columns()
            v_low(2)
            prepare_shift(0)
            for j in range(3, 6):
                v_low(j)
            dve.wait_ge(sums_ready, 2 * KC)
            link(nc.vector.tensor_tensor(row_mean[:, :], row_sum[:, 0, :], row_sum[:, 1, :], ALU.add))
            nc.vector.tensor_scalar(row_mean[:, :], row_mean[:, :], 1.0 / N, None, ALU.mult).then_inc(row_mean_done, 1)
            dve.wait_ge(row_mean_done, 1)
            nc.vector.tensor_copy(inp_hi[:, :, N], row_mean[:, :]).then_inc(row_mean_done, 1)
            dve.wait_ge(row_mean_done, 2)
            nc.vector.tensor_tensor(inp_lo[:, :, N], row_mean[:, :], inp_hi[:, :, N], ALU.subtract).then_inc(row_mean_done, 1)
            v_low(6)
            scores(0, 0)
            v_low(7)
            v_low(8)
            scores(0, 1)
            v_low(9)
            scores(0, 2)
            v_low(T - 1)
            prepare_mask(1)
            prepare_max(0)
            prepare_max(1)
            prepare_shift(1)
            tail_start(0)
            tail_middle(0)
            tail_end(0)
            dve.wait_ge(bias_done, 1)
            nc.vector.tensor_scalar(lnsb[:, :, :], lnsb[:, :, :], X_SCALE, None, ALU.mult).then_inc(ln_scaled, 1)
            low = slice(LOW, 2 * LOW)
            nc.vector.scalar_tensor_tensor(out=bias_parts[low, :], in0=bias_rows[low, :], scalar=H_SCALE * W_SCALE / CNT_SCALE, in1=bias_parts[low, :],
                                           op0=ALU.mult, op1=ALU.subtract).then_inc(bias_done, 1)
            tile(1, True)
            with dve.Fori(2, T - 2) as t:
                tile(t, True)
            tile(T - 2, True, last_next=True)
            tile(T - 1, False)
            last_tile()

        @block.tensor
        def _(pe):
            mm = nc.tensor.matmul
            pe.wait_ge(consts, 1)
            parts = [(k, h, x) for k in range(KC) for h, x in ((0, inp_hi), (0, inp_lo), (1, inp_hi))]

            def inp_transpose(t):
                pe.wait_ge(inp_ready, t + 1)
                if t >= 4:
                    pe.wait_ge(inp_l, t - 3)
                for k in range(KC):
                    ins = nc.tensor.transpose(tr_ps[t % 4][:, k * P:(k + 1) * P], inp[:, t, k * P:(k + 1) * P], ident_f[:, :])
                ins.then_inc(inp_tr, 1)

            def st_cols(t):
                pe.wait_ge(inp_l, t + 1)
                for n, (k, h, x) in enumerate(parts):
                    ins = mm(st_cols_ps[:, 2 * t:2 * t + 2], lhsT=x[:, k, t * P:(t + 1) * P], rhs=wa_parts[:, h, k, :],
                             start=(n == 0), stop=(n == len(parts) - 1))
                return ins

            def st_row(row_ps, s, c, tiles):
                n0, n1 = c * 512, min((c + 1) * 512, NP)
                pe.wait_ge(inp_l, tiles)
                for n, (k, h, x) in enumerate(parts):
                    ins = mm(row_ps[:, 0:n1 - n0], lhsT=wa_rep[:, h, k, s, :], rhs=x[:, k, n0:n1], start=(n == 0), stop=(n == len(parts) - 1))
                return ins

            for t in range(4):
                inp_transpose(t)
            pe.wait_ge(wa_ready, 1)
            st_cols(0)
            inp_transpose(4)
            st_cols(1)
            inp_transpose(5)
            st_cols(2)
            st_row(t_ps[:, 0:512], 1, 0, 4)
            inp_transpose(6)
            st_cols(3)
            inp_transpose(7)
            inp_transpose(8)
            st_cols(4)
            inp_transpose(9)
            st_cols(5)
            inp_transpose(10)
            st_row(t_ps[:, 512:1024], 1, 1, 8)
            st_row(t_ps[:, 1024:], 1, 2, T).then_inc(t_mm, 1)
            for t in range(6, T):
                ins = st_cols(t)
            ins.then_inc(st_cols_ready, 1)

            def v_tile(j):
                if j >= 4:
                    pe.wait_ge(vl_done, j - 3)
                if j == T - 3:
                    pe.wait_ge(t_rows_done, 1)
                if j == T - 1:
                    pe.wait_ge(row_mean_done, 3)
                terms = [(a, b, k) for k in range(KC) for a, b in ((inp_hi, wt_hi), (inp_hi, wt_lo), (inp_lo, wt_hi))]
                for n, (a, b, k) in enumerate(terms):
                    ins = mm(v_ps[j], lhsT=a[:, k, j * P:(j + 1) * P], rhs=b[:, k:k + KC + 1:KC, :],
                             start=(n == 0), stop=(n == len(terms) - 1))
                ins.then_inc(v_mm, 1)

            def mrow_part(t):
                pe.wait_ge(mcol_ready, t + 1)
                for s in range(2):
                    ins = nc.tensor.transpose(mrow_ps[:, s * P:(s + 1) * P], mcol[:, s, :], ident_b[:, :])
                ins.then_inc(mrow_tr, 1)

            def shifts(t, u):
                j0, n = UNITS[u]
                pe.wait_ge(mrow_ready, t + 1)
                for s in range(2):
                    after(pe, z_done[s], NU * t + u)
                    for j in range(n):
                        o = q_ps[s][:, j * P:j * P + rows(t)]
                        mm(o, lhsT=t_rows[:, j0 + j, :], rhs=mrow[:, s, 0:rows(t)], start=True, stop=False)
                        ins = mm(o, lhsT=madj[:, (j0 + j) * P:(j0 + j + 1) * P], rhs=ident_b[:, 0:rows(t)], start=False, stop=True)
                    ins.then_inc(q_ready[s], 1)

            def attend(t, u):
                j0, n = UNITS[u]
                pe.wait_ge(phi_done, NU * t + u + 1)
                if u == 0:
                    after(pe, acc_used, t)
                for s in range(2):
                    for j in range(n):
                        i = slice(j * P, (j + 1) * P)
                        mm(acc_ps[s][:, 0:VW], lhsT=p_hi[:, u, s, i], rhs=v_hi[:, j0 + j, s, 0:VW], start=(j0 + j == 0), stop=False)
                        mm(acc_ps[s][:, 0:C], lhsT=p_hi[:, u, s, i], rhs=v_lo[:, j0 + j, s, :], start=False, stop=False)
                pe.wait_ge(plo_done, NU * t + u + 1)
                for s in range(2):
                    for j in range(n):
                        ins = mm(acc_ps[s][:, 0:VW], lhsT=p_lo[:, u, s, j * P:(j + 1) * P], rhs=v_hi[:, j0 + j, s, 0:VW],
                                 start=False, stop=(j0 + j == T - 1))
                ins.then_inc(att_done, 1)

            def flat_transposes(t):
                pe.wait_ge(y_ready, t + 1)
                after(pe, pair_used, NPAIR * (t - 1) + 1)
                for k in range(KC):
                    ins = nc.tensor.transpose(f_ps[0][:, k * P:(k + 1) * P], y[:, k * P:(k + 1) * P], ident_f[:, :])
                ins.then_inc(flat_tr, 1)

            def gate_logits(t, logit_ps):
                pe.wait_ge(flat_f, KC * (t + 1))
                for k in range(KC):
                    ins = mm(logit_ps, lhsT=flat[:, k, :], rhs=gates[:, k, :], start=(k == 0), stop=(k == KC - 1))
                ins.then_inc(logits, 1)

            def hidden(t, w, first=False):
                pe.wait_ge(flat_l, t + 1)
                for half in range(2):
                    if first:
                        pe.wait_ge(pair_used, NPAIR * (t - 1) + 3)
                    elif w == 0 and isinstance(t, int) and t == T - 1:
                        pe.wait_ge(pair_used, NPAIR * t)
                    elif w == 0:
                        after(pe, pair_used, NPAIR * (t - 1) + 2 + half)
                    elif half == 0:
                        pe.wait_ge(gl_done, t + 1)
                    else:
                        after(pe, pair_used, NPAIR * t)
                    bank = f_ps[2 - 2 * w + half]
                    for c in range(KH):
                        cols = slice(half * H + c * P, half * H + (c + 1) * P)
                        terms = [(a, b, k) for k in range(KC) for a, b in ((in_hi, flat_hi), (in_hi, flat_lo), (in_lo, flat_hi))]
                        for n, (a, b, k) in enumerate(terms):
                            ins = mm(bank[:, c * P:c * P + rows(t)], lhsT=a[:, w, k, cols], rhs=b[:, k, 0:rows(t)], start=(n == 0), stop=(n == len(terms) - 1))
                ins.then_inc(in_mm[w], 1)

            def counts(t):
                pe.wait_ge(cnt_ready, t + 1)
                pe.wait_ge(hid_done[0], t + 1)
                nc.tensor.transpose(cnt_ps[:, 0:P], cnt[:, :], ident_h[:, :]).then_inc(cnt_tr, 1)

            def shared_out(t):
                pe.wait_ge(hhi_done[0], t + 1)
                pe.wait_ge(cnt_copied, t + 1)
                if isinstance(t, int) and t == T - 1:
                    pe.wait_ge(pair_used, NPAIR * t + 1)
                    o = f_ps[0][:, 0:C]
                else:
                    o = f_ps[3][:, 0:C]
                for k in range(KH):
                    mm(o, lhsT=h_hi[:, 0, k, :], rhs=so_hi[:, k, :], start=(k == 0), stop=False)
                    mm(o, lhsT=h_hi[:, 0, k, :], rhs=so_lo[:, k, :], start=False, stop=False)
                pe.wait_ge(hlo_done[0], t + 1)
                for k in range(KH):
                    mm(o, lhsT=h_lo[:, 0, k, :], rhs=so_hi[:, k, :], start=False, stop=False)
                mm(o, lhsT=cnt_t[:, :], rhs=bias_parts[:, :], start=False, stop=True).then_inc(so_mm, 1)

            def expert_pair(t, p):
                pe.wait_ge(hhi_done[1], t + 1)
                if p == 1:
                    pe.wait_ge(cnt_copied, t + 1)
                if p == 2 and isinstance(t, int) and t == T - 1:
                    pe.wait_ge(hid_done[0], t + 1)
                elif p == 2:
                    pe.wait_ge(so_used, t + 1)
                bank = f_ps[PAIR_BANK[p]]
                cols = slice(2 * p * C, (2 * p + 2) * C)
                for k in range(KH):
                    mm(bank, lhsT=h_hi[:, 1, k, :], rhs=ew[:, 0, k, cols], start=(k == 0), stop=False)
                    mm(bank, lhsT=h_hi[:, 1, k, :], rhs=ew[:, 1, k, cols], start=False, stop=False)
                pe.wait_ge(hlo_done[1], t + 1)
                for k in range(KH):
                    ins = mm(bank, lhsT=h_lo[:, 1, k, :], rhs=ew[:, 0, k, cols], start=False, stop=(k == KH - 1))
                ins.then_inc(pair_mm, 1)

            def tile(t, more):
                f = t - 1
                first = isinstance(t, int) and t == 1
                shifts(t, 0)
                if first:
                    st_row(s_rest_ps[:, 0:512], 0, 1, T)
                    st_row(s_rest_ps[:, 512:], 0, 2, T).then_inc(s_mm, 1)
                flat_transposes(f)
                if not first:
                    pe.wait_ge(mrow_ready, t + 1)
                    expert_pair(f - 1, 3)
                shifts(t, 1)
                if first:
                    pe.wait_ge(rows_done, 3)
                    low_done(pe, 1)
                    low_done(pe, 4)
                gate_logits(f, logit_ps)
                hidden(f, 0)
                attend(t, 0)
                shifts(t, 2)
                hidden(f, 1)
                counts(f)
                attend(t, 1)
                if first:
                    low_done(pe, 5)
                    pe.wait_ge(bias_done, 2)
                shared_out(f)
                attend(t, 2)
                if first:
                    low_done(pe, 9)
                    low_done(pe, 8)
                expert_pair(f, 0)
                if more and not first:
                    mrow_part(t + 1)
                expert_pair(f, 1)
                if first:
                    mrow_part(t + 1)
                if first:
                    low_done(pe, 13)
                    low_done(pe, 12)
                expert_pair(f, END_ORDER[0][2] if t_is_end(t) else 2)

            def last_tile():
                f = T - 1
                flat_transposes(f)
                expert_pair(f - 1, END_ORDER[0][3])
                hidden(f, 1, first=True)
                hidden(f, 0)
                pe.wait_ge(acc_used, T)
                gate_logits(f, last_logit_ps)
                first, second, *others = END_ORDER[1]
                expert_pair(f, first)
                expert_pair(f, second)
                counts(f)
                for p in others:
                    expert_pair(f, p)
                shared_out(f)

            low_done(pe, 0)
            v_tile(0)
            v_tile(1)
            pe.wait_ge(rows_done, 1)
            st_row(s_ps, 0, 0, 4).then_inc(s_mm, 1)
            v_tile(2)
            v_tile(3)
            v_tile(4)
            pe.wait_ge(tcols, 3)
            pe.wait_ge(rows_done, 2)
            for j in range(T):
                ins = nc.tensor.transpose(t_rows_ps[0:6, j * P:(j + 1) * P], t_parts[:, j, :], ident_b[:, :])
            ins.then_inc(t_rows_tr, 1)
            v_tile(5)
            mrow_part(0)
            v_tile(6)
            v_tile(7)
            pe.wait_ge(t_rows_done, 1)
            pe.wait_ge(vl_done, 5)
            shifts(0, 0)
            v_tile(8)
            v_tile(9)
            shifts(0, 1)
            v_tile(T - 1)
            shifts(0, 2)
            pe.wait_ge(vl_done, 9)
            attend(0, 0)
            attend(0, 1)
            pe.wait_ge(vl_done, T)
            attend(0, 2)
            mrow_part(1)
            tile(1, True)
            with pe.Fori(2, T - 1) as t:
                tile(t, True)
            tile(T - 1, False)
            last_tile()


def kernel(**inputs):
    import numpy as np
    import concourse.bacc as bacc
    from concourse.bass_utils import run_bass_kernel_spmd

    def arr(name):
        return np.asarray(inputs[name])

    laid = {
        "x": arr("x"),
        "adj": arr("adj"),
        "gat_w": arr("L0_gnn_W"),
        "gat_a": arr("L0_gnn_a").reshape(2, -1),
        "wtrans": arr("L0_gnn_wtrans"),
        "ln_pair": np.stack([arr("L0_ffn_ln_scale"), arr("L0_ffn_ln_bias")]).reshape(2, -1, P).transpose(2, 0, 1),
        "sh_in": arr("L0_ffn_shared_in_w").T,
        "sh_out": arr("L0_ffn_shared_out_w").T,
        "sh_out_b": arr("L0_ffn_shared_out_b"),
        "ex_in": arr("L0_ffn_expert_in_w").T,
        "ex_out": arr("L0_ffn_expert_out_weight").transpose(2, 0, 1),
        "ex_out_b": arr("L0_ffn_expert_out_bias"),
        "group_gate": arr("L0_ffn_group_gate_w").T,
        "expert_gate": arr("L0_ffn_expert_gate_w").T,
        "group_bias": arr("L0_ffn_group_bias"),
        "expert_bias": arr("L0_ffn_expert_bias"),
    }
    nc = bacc.Bacc("TRN2", target_bir_lowering=False, num_devices=1)
    arrays, args = {}, []
    for name, a in laid.items():
        arrays[name] = np.ascontiguousarray(a)
        args.append(nc.dram_tensor(name, a.shape, mybir.dt.from_np(a.dtype), kind="ExternalInput").ap())
    out = nc.dram_tensor("out", laid["x"].shape, F32, kind="ExternalOutput").ap()
    gnn_moe_kernel(nc, *args, out)
    r = run_bass_kernel_spmd(nc, [arrays], core_ids=[0])
    return r.results[0]["out"]
```
